# Optimizing a Trainium2 kernel written in Bass

```python
import numpy as np
import jax
import jax.numpy as jnp

def _softmax(x, axis=-1):
    return jax.nn.softmax(x, axis=axis)

def _gelu(x):
    return jax.nn.gelu(x, approximate=True)

def _silu(x):
    return jax.nn.silu(x)

def _sigmoid(x):
    return jax.nn.sigmoid(x)

def _layernorm(x, axis=-1, eps=1e-05):
    m = jnp.mean(x, axis=axis, keepdims=True)
    v = jnp.var(x, axis=axis, keepdims=True)
    return (x - m) / jnp.sqrt(v + eps)

def _scatter_add(tgt, idx, src, axis=0):
    return tgt.at[idx].add(src)

def _segment_sum(src, seg, n):
    return jax.ops.segment_sum(src, seg, n)
kernel_name = 'mk_seq_preln_d1_jaxref_r8_70b0e6'

def setup_inputs(seed: int=0):
    np.random.seed(seed)
    _w = jnp.asarray

    def _L0_attn_setup():
        import jax, jax.numpy as jnp
        import numpy as np
        B, S, E = (2, 256, 256)
        H = 16
        D = E // H

        def _rope(x):
            s, d = (x.shape[1], x.shape[3])
            pos = jnp.arange(s, dtype=jnp.float32)[:, None]
            theta = jnp.repeat(-jnp.arange(0, d, 2, dtype=jnp.float32) / d, 2)
            theta = jnp.power(10000.0, theta)
            angles = pos * theta[None, :]
            cos = jnp.cos(angles)[None, :, None, :]
            sin = jnp.sin(angles)[None, :, None, :]
            x_shift = jnp.stack((-x[..., 1::2], x[..., ::2]), axis=-1).reshape(x.shape)
            return x * cos + x_shift * sin
        key = jax.random.key(seed)
        ks = jax.random.split(key, 9)
        sc = 1.0 / np.sqrt(E)
        return {'x': jax.random.normal(ks[0], (B, S, E), jnp.float32), 'Wq': jax.random.normal(ks[1], (E, E), jnp.float32) * sc, 'bq': jax.random.normal(ks[2], (E,), jnp.float32) * 0.01, 'Wk': jax.random.normal(ks[3], (E, E), jnp.float32) * sc, 'bk': jax.random.normal(ks[4], (E,), jnp.float32) * 0.01, 'Wv': jax.random.normal(ks[5], (E, E), jnp.float32) * sc, 'bv': jax.random.normal(ks[6], (E,), jnp.float32) * 0.01, 'Wo': jax.random.normal(ks[7], (E, E), jnp.float32) * sc, 'bo': jax.random.normal(ks[8], (E,), jnp.float32) * 0.01}
    _L0_attn_in = _L0_attn_setup()

    def _L0_ffn_setup():
        import jax, jax.numpy as jnp
        import numpy as np
        B, S, H, I = (1, 64, 256, 768)

        def _quantized_matmul(x, w, scale):
            wq = w.astype(jnp.float8_e4m3fn).astype(x.dtype)
            y = jnp.einsum('bsi,io->bso', x, wq)
            return y * scale
        key = jax.random.key(seed)
        ks = jax.random.split(key, 7)
        return {'x': jax.random.normal(ks[0], (B, S, H), dtype=jnp.float32), 'gate_w': jax.random.normal(ks[1], (H, I), dtype=jnp.float32) * 0.02, 'up_w': jax.random.normal(ks[2], (H, I), dtype=jnp.float32) * 0.02, 'down_w': jax.random.normal(ks[3], (I, H), dtype=jnp.float32) * 0.02, 'gate_scale': jax.random.uniform(ks[4], (I,), dtype=jnp.float32, minval=0.5, maxval=1.5), 'up_scale': jax.random.uniform(ks[5], (I,), dtype=jnp.float32, minval=0.5, maxval=1.5), 'down_scale': jax.random.uniform(ks[6], (H,), dtype=jnp.float32, minval=0.5, maxval=1.5)}
    _L0_ffn_in = _L0_ffn_setup()
    _d = {'L0_attn_x': _L0_attn_in['x'], 'L0_attn_Wq': _L0_attn_in['Wq'], 'L0_attn_bq': _L0_attn_in['bq'], 'L0_attn_Wk': _L0_attn_in['Wk'], 'L0_attn_bk': _L0_attn_in['bk'], 'L0_attn_Wv': _L0_attn_in['Wv'], 'L0_attn_bv': _L0_attn_in['bv'], 'L0_attn_Wo': _L0_attn_in['Wo'], 'L0_attn_bo': _L0_attn_in['bo'], 'L0_ffn_gate_w': _L0_ffn_in['gate_w'], 'L0_ffn_up_w': _L0_ffn_in['up_w'], 'L0_ffn_down_w': _L0_ffn_in['down_w'], 'L0_ffn_gate_scale': _L0_ffn_in['gate_scale'], 'L0_ffn_up_scale': _L0_ffn_in['up_scale'], 'L0_ffn_down_scale': _L0_ffn_in['down_scale']}
    _x0 = _d['L0_attn_x']
    _d['L0_attn_x'] = jax.random.normal(jax.random.fold_in(jax.random.key(seed), 1), (1, 1024, 256), dtype=_x0.dtype)
    del _x0
    return _d

def reference(L0_attn_x, L0_attn_Wq, L0_attn_bq, L0_attn_Wk, L0_attn_bk, L0_attn_Wv, L0_attn_bv, L0_attn_Wo, L0_attn_bo, L0_ffn_gate_w, L0_ffn_up_w, L0_ffn_down_w, L0_ffn_gate_scale, L0_ffn_up_scale, L0_ffn_down_scale):

    def _L0_attn_ref(x, Wq, bq, Wk, bk, Wv, bv, Wo, bo):
        import jax, jax.numpy as jnp
        import numpy as np
        B, S, E = (2, 256, 256)
        H = 16
        D = E // H

        def _rope(x):
            s, d = (x.shape[1], x.shape[3])
            pos = jnp.arange(s, dtype=jnp.float32)[:, None]
            theta = jnp.repeat(-jnp.arange(0, d, 2, dtype=jnp.float32) / d, 2)
            theta = jnp.power(10000.0, theta)
            angles = pos * theta[None, :]
            cos = jnp.cos(angles)[None, :, None, :]
            sin = jnp.sin(angles)[None, :, None, :]
            x_shift = jnp.stack((-x[..., 1::2], x[..., ::2]), axis=-1).reshape(x.shape)
            return x * cos + x_shift * sin
        b, s, e = x.shape
        xq = (jnp.einsum('bse,fe->bsf', x, Wq) + bq).reshape(b, s, H, D)
        xk = (jnp.einsum('bse,fe->bsf', x, Wk) + bk).reshape(b, s, H, D)
        xv = (jnp.einsum('bse,fe->bsf', x, Wv) + bv).reshape(b, s, H, D)
        xq = _rope(xq)
        xk = _rope(xk)
        scores = jnp.einsum('bqhd,bkhd->bhqk', xq, xk) / jnp.sqrt(jnp.float32(D))
        causal = jnp.triu(jnp.ones((s, s), bool), k=1)
        scores = jnp.where(causal[None, None], -jnp.inf, scores)
        attn = jax.nn.softmax(scores, axis=-1)
        out = jnp.einsum('bhqk,bkhd->bqhd', attn, xv).reshape(b, s, e)
        return jnp.einsum('bse,fe->bsf', out, Wo) + bo

    def _L0_ffn_ref(x, gate_w, up_w, down_w, gate_scale, up_scale, down_scale):
        import jax, jax.numpy as jnp
        import numpy as np
        B, S, H, I = (1, 64, 256, 768)

        def _quantized_matmul(x, w, scale):
            wq = w.astype(jnp.float8_e4m3fn).astype(x.dtype)
            y = jnp.einsum('bsi,io->bso', x, wq)
            return y * scale
        gate = jax.nn.silu(_quantized_matmul(x, gate_w, gate_scale))
        up = _quantized_matmul(x, up_w, up_scale)
        fuse = gate * up
        return _quantized_matmul(fuse, down_w, down_scale)
    x = L0_attn_x
    x = x + _L0_attn_ref(_layernorm(x, axis=-1), L0_attn_Wq, L0_attn_bq, L0_attn_Wk, L0_attn_bk, L0_attn_Wv, L0_attn_bv, L0_attn_Wo, L0_attn_bo)
    x = x + _L0_ffn_ref(_layernorm(x, axis=-1), L0_ffn_gate_w, L0_ffn_up_w, L0_ffn_down_w, L0_ffn_gate_scale, L0_ffn_up_scale, L0_ffn_down_scale)
    return x

_drawn_inputs = setup_inputs


def setup_inputs(seed=0):
    import zlib

    import numpy as np

    out = dict(_drawn_inputs(seed))
    spreads = {}
    factors = {'L0_attn_bq': 33.177,
     'L0_attn_bk': 31.291,
     'L0_attn_bv': 5.721,
     'L0_attn_bo': 5.959,
     'L0_ffn_gate_scale': 5.342,
     'L0_ffn_up_scale': 6.194,
     'L0_ffn_down_scale': 6.024}
    for name, (base, spread) in spreads.items():
        noise = np.random.default_rng([zlib.crc32(name.encode()), seed]).standard_normal(out[name].shape)
        drawn = base * np.exp(spread * noise) if base else spread * noise
        out[name] = jnp.asarray(drawn.astype(out[name].dtype))
    for name, factor in factors.items():
        out[name] = (out[name] * factor).astype(out[name].dtype)
    return out
```

```python
import numpy as np
import concourse.bass as bass
from concourse import mybir
from concourse.alu_op_type import AluOpType as ALU
from contextlib import ExitStack

P = 128


def attention_schedule(units, pieces, exps):
    LATENCY = 5000.0
    MAX_NS, EXP_NS = 140.0, 200.0
    keyed, t = [], 0.0
    end_max = []
    for u in range(len(units)):
        for n, (_, _, _, w, _) in enumerate(pieces[u]):
            keyed.append((t, 0, ("max", u, n)))
            t += w / 0.96 + MAX_NS
        end_max.append(t)
        keyed.append((t + 1500.0, 1, ("shift", u)))
    t = 0.0
    for u in range(len(units)):
        t = max(t, end_max[u] + LATENCY)
        for n, (j, pair, q0) in enumerate(exps[u]):
            keyed.append((t, 2, ("exp", u, n)))
            t += 2 * (512 - q0) / 1.2 + EXP_NS
            if pair == 1 and j >= 1:
                keyed.append((t, 3, ("pv", u, j - 1)))
        keyed.append((t, 4, ("pv", u, exps[u][-1][0])))
        keyed.append((t + 1200.0, 5, ("norm", u)))
    return [s for _, _, s in sorted(keyed, key=lambda k: (k[0], k[1]))]


def build(nc, x, Wq, bq, Wk, bk, Wv, bv, Wo, bo, gate_w, up_w, down_w, gate_scale, up_scale,
          down_scale, cos_t, sin_t, causal, ident, bcast, out):
    fp32, bf16, fp32r, i32 = mybir.dt.float32, mybir.dt.bfloat16, mybir.dt.float32r, mybir.dt.int32
    ACT = mybir.ActivationFunctionType
    AX = mybir.AxisListType

    S, E = x.shape[1], x.shape[2]
    H, D = 16, 16
    F = gate_w.shape[1]
    T = S // P
    EK = E // P
    FK = F // P
    C = 512
    NC = S // C
    TC = C // P
    G = 4
    NG = H // G
    SCALE = 1.0 / float(np.sqrt(D))
    STACK = 6 * D
    ROWS = STACK + 2

    Q_SLOTS = [(0, 1, 3), (3, 1, 2), (5, 1, 1)]
    K_SLOTS = [(1, 2, 3), (0, 4, 2), (2, 1, 1)]

    units = [(c, g) for c in range(NC) for g in range(NG)]
    pieces = []
    for c, g in units:
        pieces.append([])
        for t in range(TC * c, TC * c + TC):
            for h in range(G):
                for k0 in range(0, (t + 1) * P, C):
                    w = min(C, (t + 1) * P - k0)
                    pieces[-1].append((h, t, k0, w, k0 + w == (t + 1) * P))
    exps = [[(j, pair, max(0, (j - TC * c) * P)) for j in range(TC * (c + 1)) for pair in range(2)]
            for c, g in units]
    first_piece = [sum(len(p) for p in pieces[:u]) for u in range(len(units) + 1)]
    first_exp = [sum(len(e) for e in exps[:u]) for u in range(len(units) + 1)]
    first_pv = [n // 2 for n in first_exp]
    schedule = attention_schedule(units, pieces, exps)

    WP = 384
    weight_pieces = []
    for m in range(2):
        weight_pieces += [(m, kt, c0) for kt in range(EK) for c0 in range(0, F, WP)]
    weight_pieces += [(2, kt, 0) for kt in range(0, FK)]

    ctx = ExitStack()
    with ctx:
        def sb(name, shape, dt=fp32, scope=ctx):
            return scope.enter_context(nc.sbuf_tensor(name, shape, dt))

        def sem(name):
            return ctx.enter_context(nc.semaphore(name))

        x_sb = sb("x_sb", [P, T, E])
        q_stack = sb("q_stack", [P, H, S], bf16)
        k_stack = sb("k_stack", [P, H, S], bf16)
        v_ones = sb("v_ones", [P, T, H, 32])
        probs = sb("probs", [P, 2, G, C])
        wo_t = sb("wo_t", [P, NG, E])
        w_gate = sb("w_gate", [P, EK, F], fp32r)
        w_up = sb("w_up", [P, EK, F], fp32r)
        w_down = sb("w_down", [P, FK, E], fp32r)
        causal_sb = sb("causal_sb", [P, C])
        ident_sb = sb("ident_sb", [P, P])
        ident_bf = sb("ident_bf", [P, P], bf16)
        bcast_sb = sb("bcast_sb", [P, P])
        down_bc = sb("down_bc", [P, E])
        gate_col = sb("gate_col", [P, FK])
        up_col = sb("up_col", [P, FK])
        half_gate = sb("half_gate", [P, FK])
        half_gu = sb("half_gu", [P, FK])
        w_raw = sb("w_raw", [P, 2, WP])
        w_exp = sb("w_exp", [P, 2, WP])
        w_chk = sb("w_chk", [P, WP])
        maxes = sb("maxes", [P, 2, 2, G * TC])
        max_all = sb("max_all", [P, 2, G * TC])
        neg_max = sb("neg_max", [P, 2, TC, 2, G], bf16)
        max_rows = sb("max_rows", [2 * G, 2, C], bf16)
        max_junk = sb("max_junk", [P, 2, C], bf16)
        stats = sb("stats", [P, 2, 6])
        mean_var = sb("mean_var", [P, 2, 2])
        var_eps = sb("var_eps", [P, 2, 1])
        rstd = sb("rstd", [P, 2, 1])
        minus_half = sb("minus_half", [P, 1])

        early = ExitStack()
        def sa(name, shape, dt=fp32):
            return sb(name, shape, dt, early)
        w_in = sa("w_in", [P, 4, EK, E])
        wo_pad = sa("wo_pad", [P, EK, H, 32])
        w_t = sa("w_t", [P, EK, 3 * E])
        bias_bc = sa("bias_bc", [P, 3 * E])
        cos_sb = sa("cos_sb", [P, T, D])
        sin_sb = sa("sin_sb", [P, T, D])
        xn = sa("xn", [P, 2, E])
        xn_t = sa("xn_t", [P, 2, EK, P])
        qk = sa("qk", [P, 2, 2 * E])
        qk_cos = sa("qk_cos", [P, 2, 2 * E])
        qk_sin = sa("qk_sin", [P, 2, 2 * E])
        qk_rot = sa("qk_rot", [P, 2, 2 * E])
        rest = sa("rest", [P, 2, 2 * E])
        part = [sa(f"part{i + 1}", [P, 2, 2 * E], bf16) for i in range(3)]
        stacked = sa("stacked", [P, 2, 2 * H, 6, D], bf16)
        early.close()
        attn_t = sb("attn_t", [P, NC, NG, C])
        o_sb = sb("o_sb", [P, 2, C])
        xn2 = sb("xn2", [P, 2, E])
        xh = sb("xh", [P, EK, C], fp32r)
        xl = sb("xl", [P, EK, C], fp32r)
        tanh_sb = sb("tanh_sb", [P, 2, C])
        gated = sb("gated", [P, 2, C])
        fuse = sb("fuse", [P, 2, C])
        fh = sb("fh", [P, 2, C], fp32r)
        fl = sb("fl", [P, 2, C], fp32r)
        scaled = sb("scaled", [P, 2, 2, E])
        out_sb = sb("out_sb", [P, 2, 2, E])

        ps = ctx.enter_context(nc.psum_tensor("ps", [P, 8, C], fp32))
        PS_EXP, PS_MAX, PS_O, PS_MISC = 0, 4, 6, 7

        x_in = [sem(f"x_in{t}") for t in range(T)]
        qkv_w_in, wo_in, bias_in, rope_in = sem("qkv_w_in"), sem("wo_in"), sem("bias_in"), sem("rope_in")
        ident_in, mask_in, scale_in, bo_in = sem("ident_in"), sem("mask_in"), sem("scale_in"), sem("bo_in")
        raw_in = [sem(f"raw_in{i}") for i in range(2)]
        filled = sem("filled")
        ident_ready = sem("ident_ready")
        pad_ready = sem("pad_ready")
        w_turned, w_copied = sem("w_turned"), sem("w_copied")
        var_ready, rstd_ready, xn_ready = sem("var_ready"), sem("rstd_ready"), sem("xn_ready")
        xn_turned, xn_copied = sem("xn_turned"), sem("xn_copied")
        qkv_done, qk_biased, v_biased = sem("qkv_done"), sem("qk_biased"), sem("v_biased")
        rope_mul, rope_done = sem("rope_mul"), sem("rope_done")
        p1_ready, rest_ready, p2_ready, p3_ready = (sem("p1_ready"), sem("rest_ready"),
                                                    sem("p2_ready"), sem("p3_ready"))
        stack_ready, stack_turned = sem("stack_ready"), sem("stack_turned")
        stack_dve, stack_act = sem("stack_dve"), sem("stack_act")
        exponent_ready, piece_rounded = sem("exponent_ready"), sem("piece_rounded")
        max_scored, max_taken = sem("max_scored"), sem("max_taken")
        neg_ready, shift_turned, shift_copied = sem("neg_ready"), sem("shift_turned"), sem("shift_copied")
        shift_in = [sem(f"shift_in{u}") for u in range(len(units))]
        scored, exp_done, masked = sem("scored"), sem("exp_done"), sem("masked")
        pv_done, o_copied, sums_done, normed = sem("pv_done"), sem("o_copied"), sem("sums_done"), sem("normed")
        projected, resid_done = sem("projected"), sem("resid_done")
        var2_ready, rstd2_ready, xn2_ready = sem("var2_ready"), sem("rstd2_ready"), sem("xn2_ready")
        xn2_turned, xh_ready, xl_ready = sem("xn2_turned"), sem("xh_ready"), sem("xl_ready")
        gu_done, tanh_done, fuse_done = sem("gu_done"), sem("tanh_done"), sem("fuse_done")
        fh_ready, fl_ready, down_done = sem("fh_ready"), sem("fl_ready"), sem("down_done")
        scaled_done, out_ready = sem("scaled_done"), sem("out_ready")
        stored = sem("stored")
        dve_step, act_step, pool_step = sem("dve_step"), sem("act_step"), sem("pool_step")

        block = ctx.enter_context(nc.Block())

        w_dst = [w_gate, w_up, w_down]

        @block.sync
        def _(sp):
            for t in range(T):
                sp.dma_start(x_sb[:, t, :], x[0, t * P:(t + 1) * P, :]).then_inc(x_in[t], 16)
                if t == 0:
                    sp.dma_start(ident_sb[:, :], ident).then_inc(ident_in, 16)
                    for i, w in enumerate((Wq, Wk, Wv)):
                        sp.dma_start(w_in[:, i, :, :], w.rearrange("(b p) e -> p b e", p=P)).then_inc(qkv_w_in, 16)
            sp.dma_start(w_in[:, 3, :, :], Wo.rearrange("(b p) e -> p b e", p=P)).then_inc(wo_in, 16)
            sp.dma_start(causal_sb[:, :], causal).then_inc(mask_in, 16)
            sp.dma_start(bcast_sb[:, :], bcast).then_inc(mask_in, 16)
            sp.dma_start(down_bc[:, :], down_scale.rearrange("(a n) -> a n", a=1).to_broadcast([P, E])).then_inc(scale_in, 16)
            sp.dma_start(gate_col[:, :], gate_scale.rearrange("(a p) -> p a", p=P),
                         allow_slow_non_contiguous=True).then_inc(scale_in, 16)
            sp.dma_start(up_col[:, :], up_scale.rearrange("(a p) -> p a", p=P),
                         allow_slow_non_contiguous=True).then_inc(scale_in, 16)
            sp.wait_ge(w_copied, 5)
            sp.dma_start(wo_t[D:D + 1, 0, :], bo.rearrange("(a n) -> a n", a=1)).then_inc(bo_in, 16)

            def load_weights(n):
                m, kt, c0 = weight_pieces[n]
                if n >= 2:
                    sp.wait_ge(piece_rounded, n - 1)
                src = (gate_w, up_w, down_w)[m]
                w = min(WP, src.shape[1] - c0)
                sp.dma_start(w_raw[:, n % 2, 0:w], src[kt * P:(kt + 1) * P, c0:c0 + w]).then_inc(raw_in[n % 2], 16)

            load_weights(0)
            load_weights(1)
            n = 2
            for u, (c, g) in enumerate(units):
                sp.wait_ge(shift_copied, u + 1)
                for p in range(2):
                    sp.dma_start(q_stack[STACK + p:STACK + p + 1, g * G:(g + 1) * G, c * C:(c + 1) * C],
                                 max_rows[p * G:(p + 1) * G, u % 2, :]).then_inc(shift_in[u], 16)
                for _ in range(2):
                    if n < len(weight_pieces):
                        load_weights(n)
                        n += 1
            assert n == len(weight_pieces)
            for c in range(NC):
                for b in range(2):
                    sp.wait_ge(out_ready, 2 * c + b + 1)
                    t = TC * c + 2 * b
                    sp.dma_start(out[0, t * P:(t + 2) * P, :].rearrange("(t p) e -> p t e", p=P),
                                 out_sb[:, b, :, :]).then_inc(stored, 16)
            sp.wait_ge(stored, 16 * 2 * NC)

        @block.gpsimd
        def _(pool):
            n_steps = [0]

            def then_wait(ins):
                n_steps[0] += 1
                ins.then_inc(pool_step, 1)
                pool.wait_ge(pool_step, n_steps[0])

            nc.gpsimd.memset(minus_half[:, :], -0.5).then_inc(filled, 1)
            then_wait(nc.gpsimd.memset(wo_pad[:, :, :, :], 0.0))
            then_wait(nc.gpsimd.memset(v_ones[:, :, :, :], 0.0))
            nc.gpsimd.memset(v_ones[:, :, :, D:D + 1], 1.0).then_inc(filled, 1)
            pool.wait_ge(filled, 2)
            nc.gpsimd.memset(k_stack[STACK:P, :, :], 1.0).then_inc(filled, 1)
            pool.wait_ge(filled, 3)
            pool.wait_ge(wo_in, 16)
            nc.gpsimd.tensor_copy(wo_pad[:, :, :, 0:D],
                                  w_in[:, 3, :, :].rearrange("p b (h d) -> p b h d", d=D)).then_inc(pad_ready, 1)

            def power(t, ready, done):
                pool.wait_ge(ready, t + 1)
                nc.gpsimd.tensor_tensor(rstd[:, t % 2, :], var_eps[:, t % 2, :], minus_half[:, :],
                                        ALU.pow).then_inc(done, 1)

            def rope(t):
                pool.wait_ge(qk_biased, t + 1)
                if t >= 2:
                    pool.wait_ge(rope_done, t - 1)
                v = qk[:, t % 2, :].rearrange("p (h i two) -> p h i two", two=2, i=D // 2)
                o = qk_sin[:, t % 2, :].rearrange("p (h i two) -> p h i two", two=2, i=D // 2)
                s = sin_sb[:, t, :].rearrange("p (i two) -> p i two", two=2)
                nc.gpsimd.tensor_tensor(qk_cos[:, t % 2, :].rearrange("p (h d) -> p h d", d=D),
                                        qk[:, t % 2, :].rearrange("p (h d) -> p h d", d=D),
                                        cos_sb[:, t, :].unsqueeze(1).to_broadcast([P, 2 * H, D]), ALU.mult)
                for a in range(2):
                    last = nc.gpsimd.tensor_tensor(o[:, :, :, a], v[:, :, :, 1 - a],
                                                   s[:, :, a].unsqueeze(1).to_broadcast([P, 2 * H, D // 2]), ALU.mult)
                last.then_inc(rope_mul, 1)

            def split(t):
                pool.wait_ge(p1_ready, t + 1)
                nc.gpsimd.tensor_tensor(rest[:, t % 2, :], qk_rot[:, t % 2, :], part[0][:, t % 2, :],
                                        ALU.subtract).then_inc(rest_ready, 1)
                pool.wait_ge(p2_ready, t + 1)
                if t >= 2:
                    pool.wait_ge(stack_ready, t - 1)
                nc.gpsimd.tensor_tensor(part[2][:, t % 2, :], rest[:, t % 2, :], part[1][:, t % 2, :],
                                        ALU.subtract).then_inc(p3_ready, 1)

            pool.wait_ge(rope_in, 32)
            for slot in range(T + 1):
                if slot < T:
                    power(slot, var_ready, rstd_ready)
                if slot >= 1:
                    rope(slot - 1)
                    split(slot - 1)

            def round_piece(n):
                m, kt, c0 = weight_pieces[n]
                w = min(WP, w_dst[m].shape[2] - c0)
                raw, e, chk = w_raw[:, n % 2, 0:w], w_exp[:, n % 2, 0:w], w_chk[:, 0:w]
                pool.wait_ge(exponent_ready, n + 1)
                then_wait(nc.gpsimd.tensor_scalar(e, e, 2.0 ** -6, 1.5 * 2.0 ** 20, ALU.max, ALU.mult))
                then_wait(nc.gpsimd.tensor_tensor(raw, raw, e, ALU.add))
                then_wait(nc.gpsimd.tensor_tensor(raw, raw, e, ALU.subtract))
                then_wait(nc.gpsimd.tensor_scalar(chk, raw, float(np.finfo(np.float32).max) / 464.0, None, ALU.mult))
                then_wait(nc.gpsimd.tensor_tensor(chk, chk, chk, ALU.subtract))
                nc.gpsimd.tensor_tensor(w_dst[m][:, kt, c0:c0 + w], raw, chk, ALU.add).then_inc(piece_rounded, 1)

            rounds = 0
            for step in schedule:
                if step[0] == "pv" and step[2] >= TC * units[step[1]][0]:
                    u, j = step[1:]
                    c, g = units[u]
                    i = j - TC * c
                    n = first_pv[u] + j
                    pool.wait_ge(exp_done, 2 * (n + 1))
                    block_ = probs[:, n % 2, :, i * P:(i + 1) * P]
                    nc.gpsimd.affine_select(out=block_, in_=block_, compare_op=ALU.is_ge, fill=0.0, base=0,
                                            pattern=[[0, G], [1, P]], channel_multiplier=-1).then_inc(masked, 1)
                if step[0] == "norm" or (step[0] == "shift"):
                    if rounds < len(weight_pieces):
                        round_piece(rounds)
                        rounds += 1
            assert rounds == len(weight_pieces)

            for c in range(NC):
                for t in range(TC * c, TC * c + TC):
                    power(t, var2_ready, rstd2_ready)
                for it in range(FK):
                    n = FK * c + it
                    pool.wait_ge(fh_ready, n + 1)
                    nc.gpsimd.tensor_tensor(fl[:, n % 2, :], fuse[:, n % 2, :], fh[:, n % 2, :].bitcast(fp32),
                                            ALU.subtract).then_inc(fl_ready, 1)
                for b in range(2):
                    t = TC * c + 2 * b
                    pool.wait_ge(scaled_done, 2 * c + b + 1)
                    if c >= 1:
                        pool.wait_ge(stored, 16 * 2 * c)
                    nc.gpsimd.tensor_tensor(out_sb[:, b, :, :], scaled[:, b, :, :], x_sb[:, t:t + 2, :],
                                            ALU.add).then_inc(out_ready, 1)

        @block.scalar
        def _(act):
            for i, b in enumerate((bq, bk, bv)):
                act.dma_start(bias_bc[:, i * E:(i + 1) * E],
                              b.rearrange("(a n) -> a n", a=1).to_broadcast([P, E])).then_inc(bias_in, 16)
            act.dma_start(cos_sb[:, :, :], cos_t.rearrange("(t p) d -> p t d", p=P)).then_inc(rope_in, 16)
            act.dma_start(sin_sb[:, :, :], sin_t.rearrange("(t p) d -> p t d", p=P)).then_inc(rope_in, 16)
            act.wait_ge(ident_in, 16)
            nc.scalar.copy(ident_bf[:, :], ident_sb[:, :]).then_inc(ident_ready, 1)
            for i in range(3):
                act.wait_ge(w_turned, i + 1)
                nc.scalar.copy(w_t[:, :, i * E:(i + 1) * E],
                               ps[:, 2 + i, :].rearrange("p (k f) -> p k f", k=EK)).then_inc(w_copied, 1)

            def xn_copy(t):
                act.wait_ge(xn_turned, t + 1)
                if t >= 2:
                    act.wait_ge(qkv_done, t - 1)
                nc.scalar.copy(xn_t[:, t % 2, :, :],
                               ps[:, t % 2, 0:EK * P].rearrange("p (k s) -> p k s", k=EK)).then_inc(xn_copied, 1)

            def parts(t):
                act.wait_ge(rope_done, t + 1)
                if t >= 2:
                    act.wait_ge(stack_ready, t - 1)
                nc.scalar.copy(part[0][:, t % 2, :], qk_rot[:, t % 2, :]).then_inc(p1_ready, 1)
                act.wait_ge(rest_ready, t + 1)
                nc.scalar.copy(part[1][:, t % 2, :], rest[:, t % 2, :]).then_inc(p2_ready, 1)

            def stack_copy(t, b):
                n = 4 * t + b
                act.wait_ge(stack_turned, n + 1)
                dst = (q_stack, k_stack)[b // 2]
                nc.scalar.copy(dst[0:STACK, 8 * (b % 2):8 * (b % 2) + 8, t * P:(t + 1) * P],
                               ps[0:STACK, 6 + n % 2, :].bitcast(bf16).rearrange("p (h s) -> p h s", h=8)
                               ).then_inc(stack_act, 1)

            for slot in range(T + 2):
                if slot < T:
                    xn_copy(slot)
                if slot >= 2:
                    stack_copy(slot - 2, 1)
                    stack_copy(slot - 2, 3)
                if slot == 1:
                    for i in range(2):
                        act.wait_ge(w_turned, 4 + i)
                        nc.scalar.copy(wo_t[:, 2 * i:2 * i + 2, :],
                                       ps[:, 5 + i, :].rearrange("p (k f) -> p k f", k=2)).then_inc(w_copied, 1)
                if 1 <= slot <= T:
                    parts(slot - 1)

            for step in schedule:
                if step[0] == "exp":
                    u, m = step[1:]
                    j, pair, q0 = exps[u][m]
                    e = first_exp[u] + m
                    n = first_pv[u] + j
                    act.wait_ge(scored, e + 1)
                    if n >= 2:
                        act.wait_ge(pv_done, n - 1)
                    nc.scalar.activation(probs[:, n % 2, 2 * pair:2 * pair + 2, q0:C],
                                         ps[:, PS_EXP + 2 * (e % 2):PS_EXP + 2 * (e % 2) + 2, q0:C],
                                         ACT.Exp, scale=SCALE).then_inc(exp_done, 1)
                if step[0] == "shift":
                    u = step[1]
                    act.wait_ge(shift_turned, u + 1)
                    if u >= 2:
                        act.wait_ge(shift_in[u - 2], 32)
                    nc.scalar.copy(max_rows[:, u % 2, :],
                                   ps[0:2 * G, PS_MISC, 0:C // 2].bitcast(bf16)).then_inc(shift_copied, 1)
                if step[0] == "norm":
                    u = step[1]
                    act.wait_ge(pv_done, first_pv[u + 1])
                    if u >= 2:
                        act.wait_ge(normed, u - 1)
                    nc.scalar.copy(o_sb[:, u % 2, :], ps[:, PS_O, :]).then_inc(o_copied, 1)

            for c in range(NC):
                for t in range(TC * c, TC * c + TC):
                    act.wait_ge(xn2_turned, t + 1)
                    if c >= 1 and t == TC * c:
                        act.wait_ge(gu_done, FK * c)
                    i = t - TC * c
                    nc.scalar.copy(xh[:, :, i * P:(i + 1) * P],
                                   ps[:, 2 + t % 2, 0:EK * P].rearrange("p (k s) -> p k s", k=EK)).then_inc(xh_ready, 1)

                def high(n):
                    act.wait_ge(fuse_done, n + 1)
                    if n >= 2:
                        act.wait_ge(down_done, n - 1)
                    nc.scalar.copy(fh[:, n % 2, :], fuse[:, n % 2, :]).then_inc(fh_ready, 1)

                for it in range(FK):
                    n = FK * c + it
                    act.wait_ge(gu_done, n + 1)
                    if n >= 2:
                        act.wait_ge(fuse_done, n - 1)
                    nc.scalar.activation(tanh_sb[:, n % 2, :], ps[:, 4 + n % 2, :], ACT.Tanh,
                                         scale=half_gate[:, it:it + 1]).then_inc(tanh_done, 1)
                    if it >= 1:
                        high(n - 1)
                high(FK * c + FK - 1)

        @block.vector
        def _(dve):
            n_steps = [0]

            def then_wait(ins):
                n_steps[0] += 1
                ins.then_inc(dve_step, 1)
                dve.wait_ge(dve_step, n_steps[0])

            def layer_norm(t, src, dst, ready, power_done, done):
                i = t % 2
                then_wait(nc.vector.bn_stats(stats[:, i, :], src))
                then_wait(nc.vector.bn_aggr(mean_var[:, i, :], stats[:, i, :]))
                nc.vector.tensor_scalar(var_eps[:, i, :], mean_var[:, i, 1:2], 1e-5, None, ALU.add).then_inc(ready, 1)
                dve.wait_ge(power_done, t + 1)
                nc.vector.tensor_scalar(dst, src, mean_var[:, i, 0:1], rstd[:, i, :],
                                        ALU.subtract, ALU.mult).then_inc(done, 1)

            def bias(t):
                i = t % 2
                dve.wait_ge(qkv_done, t + 1)
                nc.vector.tensor_tensor(qk[:, i, :], ps[:, 2 + 2 * i, :], bias_bc[:, 0:2 * E], ALU.add).then_inc(qk_biased, 1)
                nc.vector.tensor_tensor(v_ones[:, t, :, 0:D],
                                        ps[:, 3 + 2 * i, 0:E].rearrange("p (h d) -> p h d", d=D),
                                        bias_bc[:, 2 * E:3 * E].rearrange("p (h d) -> p h d", d=D), ALU.add).then_inc(v_biased, 1)

            def place(t):
                i = t % 2
                dve.wait_ge(p3_ready, t + 1)
                if t >= 2:
                    dve.wait_ge(stack_turned, 4 * (t - 1))
                for side, slots in enumerate((Q_SLOTS, K_SLOTS)):
                    for p, (first, step, count) in enumerate(slots):
                        dst = stacked[:, i, side * H:(side + 1) * H, first:first + step * (count - 1) + 1:step, :]
                        src = part[p][:, i, side * E:(side + 1) * E].rearrange("p (h d) -> p h d", d=D)
                        last = nc.vector.tensor_copy(dst, src.unsqueeze(2).to_broadcast([P, H, count, D]))
                last.then_inc(stack_ready, 1)

            def stack_copy(t, b):
                n = 4 * t + b
                dve.wait_ge(stack_turned, n + 1)
                dst = (q_stack, k_stack)[b // 2]
                nc.vector.tensor_copy(dst[0:STACK, 8 * (b % 2):8 * (b % 2) + 8, t * P:(t + 1) * P],
                                      ps[0:STACK, 6 + n % 2, :].bitcast(bf16).rearrange("p (h s) -> p h s", h=8)
                                      ).then_inc(stack_dve, 1)

            def rope_sum(t):
                i = t % 2
                dve.wait_ge(rope_mul, t + 1)
                if t >= 2:
                    dve.wait_ge(rest_ready, t - 1)
                nc.vector.tensor_tensor(qk_rot[:, i, :], qk_cos[:, i, :], qk_sin[:, i, :], ALU.add).then_inc(rope_done, 1)

            dve.wait_ge(filled, 3)
            for slot in range(T + 2):
                if slot < T:
                    dve.wait_ge(x_in[slot], 16)
                    if slot >= 2:
                        dve.wait_ge(xn_turned, slot - 1)
                    layer_norm(slot, x_sb[:, slot, :], xn[:, slot % 2, :], var_ready, rstd_ready, xn_ready)
                if slot == 1:
                    dve.wait_ge(bias_in, 48)
                if 1 <= slot <= T:
                    bias(slot - 1)
                if slot >= 2:
                    place(slot - 2)
                    stack_copy(slot - 2, 0)
                    stack_copy(slot - 2, 2)
                if 1 <= slot <= T:
                    rope_sum(slot - 1)

            dve.wait_ge(scale_in, 48)
            nc.vector.tensor_scalar(half_gate[:, :], gate_col[:, :], 0.5, None, ALU.mult)
            then_wait(nc.vector.tensor_scalar(half_gu[:, :], gate_col[:, :], 0.5, None, ALU.mult))
            then_wait(nc.vector.tensor_tensor(half_gu[:, :], half_gu[:, :], up_col[:, :], ALU.mult))

            def exponent(n):
                m, kt, c0 = weight_pieces[n]
                w = min(WP, w_dst[m].shape[2] - c0)
                dve.wait_ge(raw_in[n % 2], 16 * (n // 2 + 1))
                if n >= 2:
                    dve.wait_ge(piece_rounded, n - 1)
                nc.vector.tensor_scalar(w_exp[:, n % 2, 0:w].bitcast(i32), w_raw[:, n % 2, 0:w].bitcast(i32),
                                        0x7F800000, None, ALU.bitwise_and).then_inc(exponent_ready, 1)

            dve.wait_ge(mask_in, 32)
            exponent(0)
            exponent(1)
            n_exponents = 2
            for step in schedule:
                if step[0] == "max":
                    u, m = step[1:]
                    h, t, k0, w, diagonal = pieces[u][m]
                    n = first_piece[u] + m
                    col = (t % TC) * G + h
                    dve.wait_ge(max_scored, n + 1)
                    if diagonal:
                        nc.vector.tensor_tensor_reduce(
                            out=max_junk[:, n % 2, 0:w], in0=ps[:, PS_MAX + n % 2, 0:w], in1=causal_sb[:, C - w:C],
                            scale=1.0, scalar=-3.0e38, op0=ALU.add, op1=ALU.max,
                            accum_out=maxes[:, u % 2, k0 // C, col:col + 1]).then_inc(max_taken, 1)
                    else:
                        nc.vector.reduce_max(maxes[:, u % 2, k0 // C, col:col + 1], ps[:, PS_MAX + n % 2, 0:w],
                                             AX.X).then_inc(max_taken, 1)
                    if n + 1 == first_piece[u + 1]:
                        c, i = units[u][0], u % 2
                        dve.wait_ge(max_taken, n + 1)
                        top = maxes[:, i, 0, :]
                        if c >= 1:
                            then_wait(nc.vector.tensor_tensor(max_all[:, i, :], maxes[:, i, 0, :], maxes[:, i, 1, :], ALU.max))
                            top = max_all[:, i, :]
                        if u >= 2:
                            dve.wait_ge(shift_turned, u - 1)
                        top = top.rearrange("p (t h) -> p t h", h=G)
                        then_wait(nc.vector.tensor_scalar(neg_max[:, i, :, 0, :], top, -1.0, None, ALU.mult))
                        nc.vector.scalar_tensor_tensor(neg_max[:, i, :, 1, :], top, -1.0, neg_max[:, i, :, 0, :],
                                                       ALU.mult, ALU.subtract).then_inc(neg_ready, 1)
                if step[0] == "norm":
                    u = step[1]
                    c, g = units[u]
                    dve.wait_ge(sums_done, u + 1)
                    then_wait(nc.vector.reciprocal(ps[:, PS_MISC, :], ps[:, PS_MISC, :]))
                    nc.vector.tensor_tensor(attn_t[:, c, g, :], o_sb[:, u % 2, :], ps[:, PS_MISC, :],
                                            ALU.mult).then_inc(normed, 1)
                if step[0] in ("norm", "shift") and n_exponents < len(weight_pieces):
                    exponent(n_exponents)
                    n_exponents += 1
            assert n_exponents == len(weight_pieces)

            for c in range(NC):
                def low(t):
                    i = t - TC * c
                    dve.wait_ge(xh_ready, t + 1)
                    nc.vector.tensor_tensor(xl[:, :, i * P:(i + 1) * P],
                                            ps[:, 2 + t % 2, 0:EK * P].rearrange("p (k s) -> p k s", k=EK),
                                            xh[:, :, i * P:(i + 1) * P].bitcast(fp32), ALU.subtract).then_inc(xl_ready, 1)

                for t in range(TC * c, TC * c + TC):
                    dve.wait_ge(projected, t + 1)
                    nc.vector.tensor_tensor(x_sb[:, t, :], x_sb[:, t, :], ps[:, t % 2, 0:E], ALU.add).then_inc(resid_done, 1)
                    dve.wait_ge(resid_done, t + 1)
                    if t >= 2:
                        dve.wait_ge(xn2_turned, t - 1)
                    layer_norm(t, x_sb[:, t, :], xn2[:, t % 2, :], var2_ready, rstd2_ready, xn2_ready)
                    if t > TC * c:
                        low(t - 1)
                low(TC * c + TC - 1)
                for it in range(FK):
                    n = FK * c + it
                    dve.wait_ge(tanh_done, n + 1)
                    then_wait(nc.vector.scalar_tensor_tensor(gated[:, n % 2, :], tanh_sb[:, n % 2, :], 1.0,
                                                             ps[:, 4 + n % 2, :], ALU.add, ALU.mult))
                    if n >= 2:
                        dve.wait_ge(fl_ready, n - 1)
                    nc.vector.scalar_tensor_tensor(fuse[:, n % 2, :], gated[:, n % 2, :], half_gu[:, it:it + 1],
                                                   ps[:, 6 + n % 2, :], ALU.mult, ALU.mult).then_inc(fuse_done, 1)
                for b in range(2):
                    dve.wait_ge(down_done, FK * (c + 1))
                    if c >= 1:
                        dve.wait_ge(out_ready, 2 * c)
                    nc.vector.tensor_tensor(scaled[:, b, :, :], ps[:, b, :].rearrange("p (t e) -> p t e", t=2),
                                            down_bc[:, :].unsqueeze(1).to_broadcast([P, 2, E]), ALU.mult).then_inc(scaled_done, 1)

        @block.tensor
        def _(pe):
            pe.wait_ge(ident_in, 16)
            pe.wait_ge(qkv_w_in, 48)
            for i in range(3):
                for k in range(EK):
                    for b in range(EK):
                        o = (k * EK + b) * P
                        last = nc.tensor.transpose(ps[:, 2 + i, o:o + P], w_in[:, i, b, k * P:(k + 1) * P], ident_sb[:, :])
                last.then_inc(w_turned, 1)

            def turn_wo():
                pe.wait_ge(pad_ready, 1)
                for g in range(NG):
                    for b in range(EK):
                        o = ((g % 2) * EK + b) * P
                        last = nc.tensor.transpose(ps[:, 5 + g // 2, o:o + P],
                                                   wo_pad[:, b, g * G:(g + 1) * G, :].rearrange("p h d -> p (h d)"),
                                                   ident_sb[:, :])
                    if g % 2:
                        last.then_inc(w_turned, 1)

            def turn_xn(t):
                pe.wait_ge(xn_ready, t + 1)
                if t >= 2:
                    pe.wait_ge(xn_copied, t - 1)
                for k in range(EK):
                    last = nc.tensor.transpose(ps[:, t % 2, k * P:(k + 1) * P], xn[:, t % 2, k * P:(k + 1) * P], ident_sb[:, :])
                last.then_inc(xn_turned, 1)

            def project_qkv(t):
                pe.wait_ge(xn_copied, t + 1)
                if t == 0:
                    pe.wait_ge(w_copied, 3)
                if t == 1:
                    pe.wait_ge(w_copied, 5)
                if t >= 2:
                    pe.wait_ge(qk_biased, t - 1)
                    pe.wait_ge(v_biased, t - 1)
                for o, f0, f1 in ((2 + 2 * (t % 2), 0, 2 * E), (3 + 2 * (t % 2), 2 * E, 3 * E)):
                    for k in range(EK):
                        last = nc.tensor.matmul(ps[:, o, 0:f1 - f0], xn_t[:, t % 2, k, :], w_t[:, k, f0:f1],
                                                start=(k == 0), stop=(k == EK - 1))
                last.then_inc(qkv_done, 1)

            def turn_stacks(t):
                pe.wait_ge(stack_ready, t + 1)
                for b in range(4):
                    n = 4 * t + b
                    if n >= 2:
                        pe.wait_ge((stack_dve, stack_act)[n % 2], n // 2)
                    bank = ps[0:STACK, 6 + n % 2, :].bitcast(bf16)
                    for h in range(8):
                        last = nc.tensor.transpose(bank[:, h * P:(h + 1) * P],
                                                   stacked[:, t % 2, 8 * b + h, :, :].rearrange("p b d -> p (b d)"),
                                                   ident_bf[:, :])
                    last.then_inc(stack_turned, 1)

            for slot in range(T + 2):
                if slot < T:
                    turn_xn(slot)
                if slot == 1:
                    turn_wo()
                if slot < T:
                    project_qkv(slot)
                if slot == 0:
                    pe.wait_ge(ident_ready, 1)
                if slot >= 2:
                    turn_stacks(slot - 2)

            pe.wait_ge(stack_dve, 2 * T)
            pe.wait_ge(stack_act, 2 * T)
            pe.wait_ge(v_biased, T)
            pe.wait_ge(qk_biased, T)
            pe.wait_ge(xn_copied, T)
            pe.wait_ge(filled, 3)
            misc_free = None
            for step in schedule:
                kind, u = step[:2]
                c, g = units[u]
                if kind == "max":
                    h, t, k0, w, _ = pieces[u][step[2]]
                    n = first_piece[u] + step[2]
                    if n >= 2:
                        pe.wait_ge(max_taken, n - 1)
                    nc.tensor.matmul(ps[:, PS_MAX + n % 2, 0:w], q_stack[0:STACK, g * G + h, t * P:(t + 1) * P],
                                     k_stack[0:STACK, g * G + h, k0:k0 + w], start=True, stop=True).then_inc(max_scored, 1)
                elif kind == "shift":
                    pe.wait_ge(neg_ready, u + 1)
                    if misc_free:
                        pe.wait_ge(*misc_free)
                    for i in range(TC):
                        last = nc.tensor.transpose(ps[0:2 * G, PS_MISC, i * P // 2:(i + 1) * P // 2].bitcast(bf16),
                                                   neg_max[:, u % 2, i, :, :].rearrange("p a h -> p (a h)"), ident_bf[:, :])
                    last.then_inc(shift_turned, 1)
                    misc_free = (shift_copied, u + 1)
                elif kind == "exp":
                    j, pair, q0 = exps[u][step[2]]
                    e = first_exp[u] + step[2]
                    if step[2] == 0:
                        pe.wait_ge(shift_in[u], 32)
                    if e >= 2:
                        pe.wait_ge(exp_done, e - 1)
                    for i in range(2):
                        h = g * G + 2 * pair + i
                        last = nc.tensor.matmul(ps[:, PS_EXP + 2 * (e % 2) + i, q0:C],
                                                k_stack[0:ROWS, h, j * P:(j + 1) * P],
                                                q_stack[0:ROWS, h, c * C + q0:(c + 1) * C], start=True, stop=True)
                    last.then_inc(scored, 1)
                elif kind == "pv":
                    j = step[2]
                    n = first_pv[u] + j
                    q0 = max(0, (j - TC * c) * P)
                    pe.wait_ge(exp_done, 2 * (n + 1))
                    if j >= TC * c:
                        pe.wait_ge(masked, TC * u + j - TC * c + 1)
                    if j == 0 and u >= 1:
                        pe.wait_ge(o_copied, u)
                    for h in range(G):
                        last = nc.tensor.matmul(ps[32 * h:32 * h + 32, PS_O, q0:C], v_ones[:, j, g * G + h, :],
                                                probs[:, n % 2, h, q0:C], start=(j == 0), stop=(j == TC * (c + 1) - 1))
                    last.then_inc(pv_done, 1)
                elif kind == "norm":
                    pe.wait_ge(o_copied, u + 1)
                    if misc_free:
                        pe.wait_ge(*misc_free)
                    if u == 0:
                        pe.wait_ge(mask_in, 32)
                    nc.tensor.matmul(ps[:, PS_MISC, :], bcast_sb[:, :], o_sb[:, u % 2, :],
                                     start=True, stop=True).then_inc(sums_done, 1)
                    misc_free = (normed, u + 1)

            pe.wait_ge(normed, len(units))
            pe.wait_ge(bo_in, 16)
            pe.wait_ge(piece_rounded, len(weight_pieces))
            for c in range(NC):
                def project(t):
                    i = t - TC * c
                    if t >= 2:
                        pe.wait_ge(resid_done, t - 1)
                    if c >= 1 and i < 2:
                        pe.wait_ge(scaled_done, 2 * c)
                    for g in range(NG):
                        last = nc.tensor.matmul(ps[:, t % 2, 0:E], attn_t[:, c, g, i * P:(i + 1) * P], wo_t[:, g, :],
                                                start=(g == 0), stop=(g == NG - 1))
                    last.then_inc(projected, 1)

                def turn_xn2(t):
                    pe.wait_ge(xn2_ready, t + 1)
                    if t >= 2:
                        pe.wait_ge(xl_ready, t - 1)
                        pe.wait_ge(xh_ready, t - 1)
                    for k in range(EK):
                        last = nc.tensor.transpose(ps[:, 2 + t % 2, k * P:(k + 1) * P], xn2[:, t % 2, k * P:(k + 1) * P], ident_sb[:, :])
                    last.then_inc(xn2_turned, 1)

                for t in range(TC * c, TC * c + TC):
                    project(t)
                    if t > TC * c:
                        turn_xn2(t - 1)
                turn_xn2(TC * c + TC - 1)

                def gate_up(it):
                    n = FK * c + it
                    if n >= 2:
                        pe.wait_ge(fuse_done, n - 1)
                    for o, w in ((4, w_gate), (6, w_up)):
                        for k in range(EK):
                            for a, xs in enumerate((xh, xl)):
                                last = nc.tensor.matmul(ps[:, o + n % 2, :], w[:, k, it * P:(it + 1) * P], xs[:, k, :],
                                                        start=(k == 0 and a == 0), stop=(k == EK - 1 and a == 1))
                    last.then_inc(gu_done, 1)

                def down(it):
                    n = FK * c + it
                    pe.wait_ge(fh_ready, n + 1)
                    pe.wait_ge(fl_ready, n + 1)
                    for i in range(TC):
                        for a, fs in enumerate((fh, fl)):
                            last = nc.tensor.matmul(ps[:, i // 2, (i % 2) * E:(i % 2 + 1) * E], fs[:, n % 2, i * P:(i + 1) * P],
                                                    w_down[:, it, :], start=(it == 0 and a == 0 and i % 2 == 0),
                                                    stop=(it == FK - 1 and a == 1), skip_group_check=True)
                    last.then_inc(down_done, 1)

                pe.wait_ge(xh_ready, TC * (c + 1))
                pe.wait_ge(xl_ready, TC * (c + 1))
                for it in range(FK):
                    gate_up(it)
                    if it == 0:
                        pe.wait_ge(resid_done, TC * (c + 1))
                    if it >= 1:
                        down(it - 1)
                down(FK - 1)


_INS = ['L0_attn_x', 'L0_attn_Wq', 'L0_attn_bq', 'L0_attn_Wk', 'L0_attn_bk', 'L0_attn_Wv', 'L0_attn_bv',
        'L0_attn_Wo', 'L0_attn_bo', 'L0_ffn_gate_w', 'L0_ffn_up_w', 'L0_ffn_down_w', 'L0_ffn_gate_scale',
        'L0_ffn_up_scale', 'L0_ffn_down_scale']


def _constants():
    S, D, C = 1024, 16, 512
    pos = np.arange(S, dtype=np.float32)[:, None]
    theta = np.repeat(-np.arange(0, D, 2, dtype=np.float32) / np.float32(D), 2)
    angles = pos * np.power(np.float32(10000.0), theta)[None, :]
    sign = np.where(np.arange(D) % 2 == 0, -1.0, 1.0).astype(np.float32)
    causal = np.zeros((P, C), np.float32)
    causal[:, C - P:] = np.where(np.arange(P)[None, :] > np.arange(P)[:, None], -3.0e38, 0.0)
    bcast = np.zeros((P, P), np.float32)
    for h in range(4):
        bcast[32 * h + D, 32 * h:32 * h + 32] = 1.0
    return {"cos": np.cos(angles), "sin": np.sin(angles) * sign, "causal": causal,
            "ident": np.eye(P, dtype=np.float32), "bcast": bcast}


def kernel(**inputs):
    import concourse.bacc as _bacc
    from concourse.bass_utils import run_bass_kernel_spmd as _run

    nc = _bacc.Bacc("TRN2", target_bir_lowering=False, num_devices=1)
    arrays, args = {}, []
    for name, a in [(n, inputs[n]) for n in _INS] + list(_constants().items()):
        a = np.ascontiguousarray(a)
        arrays[f"in_{name}_dram"] = a
        args.append(nc.dram_tensor(f"in_{name}_dram", a.shape, mybir.dt.from_np(a.dtype), kind="ExternalInput").ap())
    out = nc.dram_tensor("out_0_dram", (1, 1024, 256), mybir.dt.float32, kind="ExternalOutput").ap()
    build(nc, *args, out)
    r = _run(nc, [arrays], core_ids=[0])
    return r.results[0]["out_0_dram"]
```

```python
import numpy as np
import concourse.bass as bass
from concourse import mybir
from concourse.alu_op_type import AluOpType as ALU
from contextlib import ExitStack

P = 128


PATIENCE = {
    'tensor': 400, 'gpsimd': 200, 'scalar': 400, 'vector': 200,
}
FAVOUR = {
    'bias': -3000, 'max': -3000, 'fuse': -10000, 'o_copy': 80000, 'rest': 3000, 'fh': 1000,
    'qkv': -10000, 'stats': 3000, 'rounded': -1000, 'turn_stack': -3000, 'check': -40000,
    'mask': 3000, 'norm': 3000, 'rope': -80000, 'exponent': 1000, 'place': -10000, 'exp': -20000,
    'taken': 1000, 'bo': -5000, 'xn': -5000, 'stack_act': -10000, 'shift': 5000, 'resid': -5000,
    'project': 1000, 'stack_dve': 3000,
}


class Plan:

    HOP, HOP_TO_PE = 200.0, 290.0

    def __init__(self, patience, favour):
        self.steps, self.last = {}, {}
        self.patience, self.favour = patience, favour

    def add(self, step, engine, ns, after=(), banks=0, keeps=False, frees=None, late=0.0):
        kind = step[0]
        after = [a for a in (*after, self.last.get(kind)) if a is not None]
        self.steps[step] = (engine, ns, after, banks, frees, late)
        self.last[kind] = step

    @staticmethod
    def choose(bank_free, banks, t):
        if banks == 2:
            pairs = [(max(t, bank_free[b][0], bank_free[b + 1][0]), b) for b in range(0, 8, 2)
                     if b in bank_free and b + 1 in bank_free]
            return [min(pairs)[1], min(pairs)[1] + 1] if pairs else None
        singles = [(max(t, bank_free[b][0]), b ^ 1 in bank_free, b) for b in bank_free]
        return [min(singles)[2]] if singles else None

    def solve(self):
        steps = self.steps
        behind, users = {}, {k: [] for k in steps}
        for k, (_, _, after, _, _, _) in steps.items():
            for a in after:
                users[a].append(k)
        todo = {k: len(v[2]) for k, v in steps.items()}
        topo = [k for k in steps if not todo[k]]
        for k in topo:
            for u in users[k]:
                todo[u] -= 1
                if not todo[u]:
                    topo.append(u)
        assert len(topo) == len(steps), "a circle of steps"
        for k in reversed(topo):
            behind[k] = steps[k][1] + steps[k][5] + max([behind[u] for u in users[k]], default=0.0)
        todo = {k: len(v[2]) for k, v in steps.items()}
        ready = {k for k in steps if not todo[k]}
        end, free_at = {}, {}
        bank_free = {b: (0.0, None) for b in range(8)}
        held = {}
        order, banks_of, former = {}, {}, {}
        while ready:
            starts = {}
            for k in ready:
                engine, ns, after, banks, frees, late = steps[k]
                t = free_at.get(engine, 0.0)
                for a in after:
                    hop = 0.0 if steps[a][0] == engine else self.HOP_TO_PE if engine == "tensor" else self.HOP
                    t = max(t, end[a] + hop)
                if banks:
                    mine = self.choose(bank_free, banks, t)
                    if mine is None:
                        continue
                    t = max(t, max(bank_free[b][0] for b in mine))
                starts[k] = t
            assert starts, "no step can start"
            first = min(starts, key=lambda k: (starts[k], str(k)))
            rivals = [k for k in starts if steps[k][0] == steps[first][0]
                      and starts[k] <= starts[first] + self.patience.get(steps[k][0], 0.0)]
            k = max(rivals, key=lambda k: (behind[k] + self.favour.get(k[0], 0.0), -starts[k], str(k)))
            t = starts[k]
            engine, ns, after, banks, frees, late = steps[k]
            ready.discard(k)
            if banks:
                mine = self.choose(bank_free, banks, t)
                former[k] = [bank_free.pop(b)[1] for b in mine]
                banks_of[k] = held[k] = mine
            order.setdefault(engine, []).append(k)
            free_at[engine] = t + ns
            end[k] = t + ns + late
            if frees is not None:
                for b in held.pop(frees):
                    bank_free[b] = (end[k] + self.HOP, k)
            for u in users[k]:
                todo[u] -= 1
                if not todo[u]:
                    ready.add(u)
        return order, banks_of, former, max(end.values())


def plan_steps(T, TC, NG, G, FK, C, units, pieces, exps, first_piece, first_exp, first_pv, weight_pieces):
    p = Plan(PATIENCE, FAVOUR)
    ROUND_AT = 60000.0
    U, NC = len(units), T // TC

    def at(kind, n):
        return (kind, n) if n >= 0 else None

    for t in range(T):
        p.add(("x_in", t), f"dma_x{t}", 2700.0 + 1500.0 * min(t, 4))
    for i in range(4):
        p.add(("w_in", i), f"dma_w{i}", 4300.0 + 1500.0 * i)
    for i in range(3):
        p.add(("turn_w", i), "tensor", 700.0, [("w_in", i)], banks=1)
        p.add(("w_copy", i), "scalar", 478.0, [("turn_w", i)], frees=("turn_w", i))
    p.add(("turn_w", 3), "tensor", 430.0, [("w_in", 3)], banks=1)
    p.add(("w_copy", 3), "scalar", 478.0, [("turn_w", 3), ("w_copy", 2)], frees=("turn_w", 3))
    for t in range(T):
        p.add(("stats", t), "vector", 735.0, [("x_in", t), at("xn", t - 2)])
        p.add(("power", t), "gpsimd", 464.0, [("stats", t)])
        p.add(("xn", t), "vector", 323.0, [("power", t), at("turn_xn", t - 4)])
        p.add(("bo", t), "gpsimd", 687.0, [("xn", t), at("bo", t - 1)])
        p.add(("turn_xn", t), "tensor", 220.0, [("xn", t)], banks=1)
        p.add(("xn_copy", t), "scalar", 264.0, [("turn_xn", t), at("qkv", t - 4)], frees=("turn_xn", t))
        p.add(("qkv", t), "tensor", 2600.0, [("xn_copy", t), ("w_copy", 2)], banks=2)
        p.add(("bias", t), "vector", 940.0, [("qkv", t), at("rope", t - 2)], frees=("qkv", t))
        p.add(("rope", t), "gpsimd", 2830.0, [("bias", t), at("rope_sum", t - 2)])
        p.add(("rope_sum", t), "vector", 600.0, [("rope", t), at("rest", t - 2)])
        p.add(("p1", t), "scalar", 520.0, [("rope_sum", t), at("place", t - 2)])
        p.add(("rest", t), "vector", 600.0, [("p1", t), at("p3", t - 2)])
        p.add(("p2", t), "scalar", 520.0, [("rest", t)])
        p.add(("p3", t), "gpsimd", 1113.0, [("p2", t)])
        p.add(("place", t), "vector", 1250.0, [("p3", t), at("turn_stack", 4 * (t - 2) + 3)])
        for b in range(4):
            n = 4 * t + b
            p.add(("turn_stack", n), "tensor", 450.0, [("place", t), at("turn_stack", n - 1)], banks=1)
            if b == 0:
                p.add(("stack_dve", t), "vector", 600.0, [("turn_stack", n)], frees=("turn_stack", n))
            else:
                p.add(("stack_act", 3 * t + b - 1), "scalar", 904.0, [("turn_stack", n), at("stack_act", 3 * t + b - 2)],
                      frees=("turn_stack", n))
    N = len(weight_pieces)
    p.add(("rounding_begins", 0), "clock", ROUND_AT)
    for n in range(N):
        p.add(("raw", n), "sync", 100.0, [at("rounded", n - 2), ("rounding_begins", 0)], late=2500.0)
        p.add(("exponent", n), "vector", 610.0, [("raw", n)])
        p.add(("round", n), "gpsimd", 1780.0, [("exponent", n)])
        p.add(("check", n), "vector", 240.0, [("round", n), at("rounded", n - 1)])
        p.add(("rounded", n), "gpsimd", 841.0, [("check", n)])
    for u, (c, g) in enumerate(units):
        last_stack = TC * (c + 1) - 1
        for m, (_, _, _, w, _) in enumerate(pieces[u]):
            n = first_piece[u] + m
            p.add(("max", u, m), "tensor", w / 2.4 + 3.0,
                  [("stack_act", 3 * last_stack + 2), ("stack_dve", last_stack), flat(pieces, first_piece, n - 1, "max"),
                   flat(pieces, first_piece, n - 2, "taken")], banks=1)
            p.add(("taken", u, m), "vector", w / 0.96 + 70.0, [("max", u, m), at("neg", u - 2)], frees=("max", u, m))
        p.add(("neg", u), "vector", 520.0, [("taken", u, len(pieces[u]) - 1), at("shift", u - 2)])
        p.add(("shift", u), "tensor", 150.0, [("neg", u)], banks=1)
        p.add(("shift_copy", u), "scalar", 478.0, [("shift", u), at("shift_in", u - 2)], frees=("shift", u))
        p.add(("shift_in", u), "sync", 200.0, [("shift_copy", u)], late=2300.0)
        for m, (j, pair, q0) in enumerate(exps[u]):
            e, n = first_exp[u] + m, first_pv[u] + j
            p.add(("score", u, m), "tensor", 2 * (C - q0) / 2.4 + 6.0,
                  [("shift_in", u), ("stack_act", 3 * T - 1), ("stack_dve", T - 1), flat(exps, first_exp, e - 1, "score"),
                   flat(exps, first_exp, e - 2, "exp")], banks=2)
            p.add(("exp", u, m), "scalar", 2 * (C - q0) / 1.2 + 51.0,
                  [("score", u, m), flat([e[::2] for e in exps], first_pv, n - 2, "pv")], frees=("score", u, m))
            if pair == 1:
                if j >= TC * c:
                    p.add(("mask", u, j), "gpsimd", 600.0, [("exp", u, m)])
                p.add(("pv", u, j), "tensor", 940.0 * (C - q0) / C,
                      [("exp", u, m), ("mask", u, j) if j >= TC * c else None, ("o_copy", u - 1) if u and j == 0 else None],
                      banks=1 if j == 0 else 0)
        p.add(("o_copy", u), "scalar", 478.0, [("pv", u, exps[u][-1][0]), at("turn_o", u - 2)], frees=("pv", u, 0))
        p.add(("turn_o", u), "tensor", 440.0, [("o_copy", u)], banks=1)
        p.add(("norm", u), "vector", 630.0, [("turn_o", u), at("norm", u - 1)], frees=("turn_o", u))
    for t in range(T):
        c = t // TC
        p.add(("turn_attn", t), "tensor", 220.0, [("norm", NG * (c + 1) - 1)], banks=1)
        p.add(("attn_copy", t), "scalar", 264.0, [("turn_attn", t), at("project", t - 2)], frees=("turn_attn", t))
        p.add(("project", t), "tensor", 880.0, [("attn_copy", t), ("w_copy", 3)], banks=1)
        p.add(("resid", t), "vector", 335.0, [("project", t), ("bo", T - 1)], frees=("project", t))
        p.add(("stats2", t), "vector", 860.0, [("resid", t), at("xn2", t - 2)])
        p.add(("power2", t), "gpsimd", 464.0, [("stats2", t)])
        p.add(("xn2", t), "vector", 323.0, [("power2", t), at("turn_xn2", t - 2)])
        p.add(("turn_xn2", t), "tensor", 220.0, [("xn2", t)], banks=1)
        free = [("gate_up", FK * c - 1)] if c else []
        p.add(("xh", t), "scalar", 264.0, [("turn_xn2", t)] + free)
        p.add(("xl", t), "vector", 335.0, [("xh", t)], frees=("turn_xn2", t))
    for n in range(FK * NC):
        c, it = divmod(n, FK)
        p.add(("gate_up", n), "tensor", 1730.0, [("xl", TC * (c + 1) - 1), ("rounded", N - 1), at("fuse", n - 2)], banks=2)
        p.add(("tanh", n), "scalar", 571.0, [("gate_up", n), at("fuse", n - 2)])
        p.add(("fuse", n), "vector", 1395.0, [("tanh", n), at("fl", n - 2)], frees=("gate_up", n))
        p.add(("fh", n), "scalar", 520.0, [("fuse", n), at("down", n - 2)])
        p.add(("fl", n), "gpsimd", 1225.0, [("fh", n)])
        p.add(("down", n), "tensor", 900.0, [("fl", n), at("scaled", 2 * c - 1) if it == 0 else None],
              banks=2 if it == 0 else 0)
    for c in range(NC):
        for b in range(2):
            k = 2 * c + b
            p.add(("scaled", k), "vector", 600.0, [("down", FK * (c + 1) - 1), at("out", k - 2)],
                  frees=("down", FK * c) if b else None)
            p.add(("out", k), "gpsimd", 1225.0, [("scaled", k), at("store", k - 2)])
            p.add(("store", k), "sync", 100.0, [("out", k)], late=2300.0)
    return p.solve()


def flat(lists, first, n, kind):
    if n < 0:
        return None
    u = max(i for i in range(len(lists)) if first[i] <= n)
    if kind == "pv":
        return (kind, u, n - first[u])
    return (kind, u, n - first[u])


def build(nc, x, Wq, bq, Wk, bk, Wv, bv, Wo, bo, gate_w, up_w, down_w, gate_scale, up_scale,
          down_scale, cos_t, sin_t, causal, ident, out):
    fp32, bf16, fp32r, i32 = mybir.dt.float32, mybir.dt.bfloat16, mybir.dt.float32r, mybir.dt.int32
    ACT = mybir.ActivationFunctionType
    AX = mybir.AxisListType

    S, E = x.shape[1], x.shape[2]
    H, D = 16, 16
    F = gate_w.shape[1]
    T = S // P
    EK = E // P
    FK = F // P
    C = 512
    NC = S // C
    TC = C // P
    G = 4
    NG = H // G
    SCALE = 1.0 / float(np.sqrt(D))
    STACK = 6 * D
    ROWS = STACK + 2

    X_LOADS = [(0, 1), (1, 2), (2, 4), (4, T)]
    Q_SLOTS = [(0, 1, 3), (3, 1, 2), (5, 1, 1)]
    K_SLOTS = [(1, 2, 3), (0, 4, 2), (2, 1, 1)]

    units = [(c, g) for c in range(NC) for g in range(NG)]
    pieces = []
    for c, g in units:
        pieces.append([])
        for t in range(TC * c, TC * c + TC):
            for h in range(G):
                for k0 in range(0, (t + 1) * P, C):
                    w = min(C, (t + 1) * P - k0)
                    pieces[-1].append((h, t, k0, w, k0 + w == (t + 1) * P))
    exps = [[(j, pair, max(0, (j - TC * c) * P)) for j in range(TC * (c + 1)) for pair in range(2)]
            for c, g in units]
    first_piece = [sum(len(p) for p in pieces[:u]) for u in range(len(units) + 1)]
    first_exp = [sum(len(e) for e in exps[:u]) for u in range(len(units) + 1)]
    first_pv = [n // 2 for n in first_exp]

    WP = 384
    weight_pieces = []
    for m in range(2):
        weight_pieces += [(m, kt, c0) for kt in range(EK) for c0 in range(0, F, WP)]
    weight_pieces += [(2, kt, 0) for kt in range(0, FK)]

    order, banks_of, former, _ = plan_steps(T, TC, NG, G, FK, C, units, pieces, exps,
                                            first_piece, first_exp, first_pv, weight_pieces)

    ctx = ExitStack()
    with ctx:
        def sb(name, shape, dt=fp32, scope=ctx):
            return scope.enter_context(nc.sbuf_tensor(name, shape, dt))

        def sem(name):
            return ctx.enter_context(nc.semaphore(name))

        x_sb = sb("x_sb", [P, T, E])
        q_stack = sb("q_stack", [P, H, S], bf16)
        k_stack = sb("k_stack", [P, H, S], bf16)
        v_ones = sb("v_ones", [P, T, H, 32])
        probs = sb("probs", [P, 2, G, C])
        wo_t = sb("wo_t", [P, EK, E])
        w_gate = sb("w_gate", [P, EK, F], fp32r)
        w_up = sb("w_up", [P, EK, F], fp32r)
        w_down = sb("w_down", [P, FK, E], fp32r)
        causal_sb = sb("causal_sb", [P, C])
        ident_sb = sb("ident_sb", [P, P])
        ident_bf = sb("ident_bf", [P, P], bf16)
        ones_row = sb("ones_row", [2, S], bf16)
        bo_bc = sb("bo_bc", [P, E])
        down_bc = sb("down_bc", [P, E])
        gate_col = sb("gate_col", [P, FK])
        up_col = sb("up_col", [P, FK])
        half_gate = sb("half_gate", [P, FK])
        half_gu = sb("half_gu", [P, FK])
        w_raw = sb("w_raw", [P, 2, WP])
        w_exp = sb("w_exp", [P, 2, WP])
        w_chk = sb("w_chk", [P, WP])
        maxes = sb("maxes", [P, 2, 2, G * TC])
        max_all = sb("max_all", [P, 2, G * TC])
        neg_max = sb("neg_max", [P, 2, TC, 2, G], bf16)
        max_rows = sb("max_rows", [2 * G, 2, C], bf16)
        max_junk = sb("max_junk", [P, 2, C], bf16)
        stats = sb("stats", [P, 2, 6])
        mean_var = sb("mean_var", [P, 2, 2])
        var_eps = sb("var_eps", [P, 2, 1])
        rstd = sb("rstd", [P, 2, 1])
        stats2 = sb("stats2", [P, 2, 6])
        mean_var2 = sb("mean_var2", [P, 2, 2])
        var_eps2 = sb("var_eps2", [P, 2, 1])
        rstd2 = sb("rstd2", [P, 2, 1])
        minus_half = sb("minus_half", [P, 1])
        inv_sum = sb("inv_sum", [P, 2, TC, G])

        early = ExitStack()

        def sa(name, shape, dt=fp32):
            return sb(name, shape, dt, early)
        w_in = sa("w_in", [P, 4, EK, E])
        w_t = sa("w_t", [P, EK, 3 * E])
        bias_bc = sa("bias_bc", [P, 3 * E])
        cos_sb = sa("cos_sb", [P, T, D])
        sin_sb = sa("sin_sb", [P, T, D])
        xn = sa("xn", [P, 4, E])
        xn_t = sa("xn_t", [P, 4, EK, P])
        qk = sa("qk", [P, 2, 2 * E])
        qk_cos = sa("qk_cos", [P, 2, 2 * E])
        qk_sin = sa("qk_sin", [P, 2, 2 * E])
        qk_rot = sa("qk_rot", [P, 2, 2 * E])
        rest = sa("rest", [P, 2, 2 * E])
        part = [sa(f"part{i + 1}", [P, 2, 2 * E], bf16) for i in range(3)]
        stacked = sa("stacked", [P, 2, 2 * H, 6, D], bf16)
        early.close()
        o_sb = sb("o_sb", [P, 2, C])
        attn_s = sb("attn_s", [P, T, E])
        attn_t = sb("attn_t", [P, 2, EK, P])
        xn2 = sb("xn2", [P, 2, E])
        xh = sb("xh", [P, EK, C], fp32r)
        xl = sb("xl", [P, EK, C], fp32r)
        tanh_sb = sb("tanh_sb", [P, 2, C])
        gated = sb("gated", [P, 2, C])
        fuse = sb("fuse", [P, 2, C])
        fh = sb("fh", [P, 2, C], fp32r)
        fl = sb("fl", [P, 2, C], fp32r)
        scaled = sb("scaled", [P, 2, 2, E])
        out_sb = sb("out_sb", [P, 2, 2, E])

        ps = ctx.enter_context(nc.psum_tensor("ps", [P, 8, C], fp32))

        x_in = [sem(f"x_in{n}") for n in range(len(X_LOADS))]
        qkv_w_in = [sem(f"qkv_w_in{i}") for i in range(3)]
        wo_in, bias_in, rope_in = sem("wo_in"), sem("bias_in"), sem("rope_in")
        ident_in, mask_in, scale_in, bo_in, ones_in = (sem("ident_in"), sem("mask_in"), sem("scale_in"),
                                                       sem("bo_in"), sem("ones_in"))
        raw_in = [sem(f"raw_in{i}") for i in range(2)]
        shift_in = [sem(f"shift_in{u}") for u in range(len(units))]
        stored = [sem(f"stored{k}") for k in range(2 * NC)]
        half_set, ones_set, v_pads_set, ident_ready = (sem("half_set"), sem("ones_set"), sem("v_pads_set"),
                                                       sem("ident_ready"))
        w_turned, w_copied = sem("w_turned"), sem("w_copied")
        var_ready, rstd_ready, xn_ready, bo_added = sem("var_ready"), sem("rstd_ready"), sem("xn_ready"), sem("bo_added")
        xn_turned, xn_copied, qkv_done = sem("xn_turned"), sem("xn_copied"), sem("qkv_done")
        qk_biased, v_biased = sem("qk_biased"), sem("v_biased")
        rope_mul, rope_done = sem("rope_mul"), sem("rope_done")
        p1_ready, rest_ready, p2_ready, p3_ready = (sem("p1_ready"), sem("rest_ready"),
                                                    sem("p2_ready"), sem("p3_ready"))
        placed, stack_turned = sem("placed"), sem("stack_turned")
        stack_dve, stack_act = sem("stack_dve"), sem("stack_act")
        exponent_ready, piece_cut, piece_checked, piece_rounded = (sem("exponent_ready"), sem("piece_cut"),
                                                                   sem("piece_checked"), sem("piece_rounded"))
        max_scored, max_taken = sem("max_scored"), sem("max_taken")
        neg_ready, shift_turned, shift_copied = sem("neg_ready"), sem("shift_turned"), sem("shift_copied")
        scored, exp_done, masked = sem("scored"), sem("exp_done"), sem("masked")
        pv_done, o_copied, o_turned, normed = sem("pv_done"), sem("o_copied"), sem("o_turned"), sem("normed")
        attn_turned, attn_copied = sem("attn_turned"), sem("attn_copied")
        projected, resid_done = sem("projected"), sem("resid_done")
        var2_ready, rstd2_ready, xn2_ready = sem("var2_ready"), sem("rstd2_ready"), sem("xn2_ready")
        xn2_turned, xh_ready, xl_ready = sem("xn2_turned"), sem("xh_ready"), sem("xl_ready")
        gu_done, tanh_done, fuse_done = sem("gu_done"), sem("tanh_done"), sem("fuse_done")
        fh_ready, fl_ready, down_done = sem("fh_ready"), sem("fl_ready"), sem("down_done")
        scaled_done, out_ready = sem("scaled_done"), sem("out_ready")
        dve_step = sem("dve_step")

        block = ctx.enter_context(nc.Block())

        w_dst = [w_gate, w_up, w_down]
        piece_width = [min(WP, w_dst[m].shape[2] - c0) for m, _, c0 in weight_pieces]

        @block.sync
        def _(sp):
            for n, (t0, t1) in enumerate(X_LOADS):
                sp.dma_start(x_sb[:, t0:t1, :], x[0, t0 * P:t1 * P, :].rearrange("(t p) e -> p t e", p=P)
                             ).then_inc(x_in[n], 16)
                if n < 3:
                    sp.dma_start(w_in[:, n, :, :], (Wq, Wk, Wv)[n].rearrange("(b p) e -> p b e", p=P)
                                 ).then_inc(qkv_w_in[n], 16)
            sp.dma_start(w_in[:, 3, :, :], Wo.rearrange("(b p) e -> p b e", p=P)).then_inc(wo_in, 16)
            sp.dma_start(causal_sb[:, :], causal).then_inc(mask_in, 16)
            sp.wait_ge(ones_set, 1)
            sp.dma_start(k_stack[STACK:ROWS, :, :],
                         ones_row[:, :].unsqueeze(1).to_broadcast([2, H, S])).then_inc(ones_in, 16)
            for step in order["sync"]:
                kind, n = step
                if kind == "raw":
                    m, kt, c0 = weight_pieces[n]
                    if n >= 2:
                        sp.wait_ge(piece_rounded, n - 1)
                    sp.dma_start(w_raw[:, n % 2, 0:piece_width[n]],
                                 (gate_w, up_w, down_w)[m][kt * P:(kt + 1) * P, c0:c0 + piece_width[n]]
                                 ).then_inc(raw_in[n % 2], 16)
                elif kind == "shift_in":
                    c, g = units[n]
                    sp.wait_ge(shift_copied, n + 1)
                    for p in range(2):
                        sp.dma_start(q_stack[STACK + p:STACK + p + 1, g * G:(g + 1) * G, c * C:(c + 1) * C],
                                     max_rows[p * G:(p + 1) * G, n % 2, :]).then_inc(shift_in[n], 16)
                elif kind == "store":
                    t = 2 * n
                    sp.wait_ge(out_ready, n + 1)
                    sp.dma_start(out[0, t * P:(t + 2) * P, :].rearrange("(t p) e -> p t e", p=P),
                                 out_sb[:, n % 2, :, :]).then_inc(stored[n], 16)
            for s in stored:
                sp.wait_ge(s, 16)

        @block.gpsimd
        def _(pool):
            nc.gpsimd.memset(minus_half[:, :], -0.5).then_inc(half_set, 1)
            pool.wait_ge(half_set, 1)
            nc.gpsimd.memset(ones_row[:, :], 1.0).then_inc(ones_set, 1)
            pool.wait_ge(ones_set, 1)
            for step in order["gpsimd"]:
                kind, n = step[:2]
                if kind == "power":
                    pool.wait_ge(var_ready, n + 1)
                    nc.gpsimd.tensor_tensor(rstd[:, n % 2, :], var_eps[:, n % 2, :], minus_half[:, :],
                                            ALU.pow).then_inc(rstd_ready, 1)
                elif kind == "bo":
                    if n == 0:
                        pool.wait_ge(bo_in, 16)
                    pool.wait_ge(xn_ready, n + 1)
                    nc.gpsimd.tensor_tensor(x_sb[:, n, :], x_sb[:, n, :], bo_bc[:, :], ALU.add).then_inc(bo_added, 1)
                elif kind == "rope":
                    if n == 0:
                        pool.wait_ge(rope_in, 32)
                    pool.wait_ge(qk_biased, n + 1)
                    if n >= 2:
                        pool.wait_ge(rope_done, n - 1)
                    v = qk[:, n % 2, :].rearrange("p (h i two) -> p h i two", two=2, i=D // 2)
                    o = qk_sin[:, n % 2, :].rearrange("p (h i two) -> p h i two", two=2, i=D // 2)
                    s = sin_sb[:, n, :].rearrange("p (i two) -> p i two", two=2)
                    nc.gpsimd.tensor_tensor(qk_cos[:, n % 2, :].rearrange("p (h d) -> p h d", d=D),
                                            qk[:, n % 2, :].rearrange("p (h d) -> p h d", d=D),
                                            cos_sb[:, n, :].unsqueeze(1).to_broadcast([P, 2 * H, D]), ALU.mult)
                    for a in range(2):
                        last = nc.gpsimd.tensor_tensor(o[:, :, :, a], v[:, :, :, 1 - a],
                                                       s[:, :, a].unsqueeze(1).to_broadcast([P, 2 * H, D // 2]), ALU.mult)
                    last.then_inc(rope_mul, 1)
                elif kind == "p3":
                    pool.wait_ge(p2_ready, n + 1)
                    if n >= 2:
                        pool.wait_ge(placed, n - 1)
                    nc.gpsimd.tensor_tensor(part[2][:, n % 2, :], rest[:, n % 2, :], part[1][:, n % 2, :],
                                            ALU.subtract).then_inc(p3_ready, 1)
                elif kind == "round":
                    raw, e = w_raw[:, n % 2, 0:piece_width[n]], w_exp[:, n % 2, 0:piece_width[n]]
                    pool.wait_ge(exponent_ready, n + 1)
                    nc.gpsimd.tensor_tensor(raw, raw, e, ALU.add).then_inc(piece_cut, 1)
                    pool.wait_ge(piece_cut, 2 * n + 1)
                    nc.gpsimd.tensor_tensor(raw, raw, e, ALU.subtract).then_inc(piece_cut, 1)
                elif kind == "rounded":
                    m, kt, c0 = weight_pieces[n]
                    w = piece_width[n]
                    pool.wait_ge(piece_checked, n + 1)
                    nc.gpsimd.tensor_tensor(w_dst[m][:, kt, c0:c0 + w], w_raw[:, n % 2, 0:w], w_chk[:, 0:w],
                                            ALU.add).then_inc(piece_rounded, 1)
                elif kind == "mask":
                    u, j = step[1:]
                    c, g = units[u]
                    i = j - TC * c
                    k = first_pv[u] + j
                    pool.wait_ge(exp_done, 2 * (k + 1))
                    block_ = probs[:, k % 2, :, i * P:(i + 1) * P]
                    nc.gpsimd.affine_select(out=block_, in_=block_, compare_op=ALU.is_ge, fill=0.0, base=0,
                                            pattern=[[0, G], [1, P]], channel_multiplier=-1).then_inc(masked, 1)
                elif kind == "power2":
                    pool.wait_ge(var2_ready, n + 1)
                    nc.gpsimd.tensor_tensor(rstd2[:, n % 2, :], var_eps2[:, n % 2, :], minus_half[:, :],
                                            ALU.pow).then_inc(rstd2_ready, 1)
                elif kind == "fl":
                    pool.wait_ge(fh_ready, n + 1)
                    nc.gpsimd.tensor_tensor(fl[:, n % 2, :], fuse[:, n % 2, :], fh[:, n % 2, :].bitcast(fp32),
                                            ALU.subtract).then_inc(fl_ready, 1)
                elif kind == "out":
                    pool.wait_ge(scaled_done, n + 1)
                    if n >= 2:
                        pool.wait_ge(stored[n - 2], 16)
                    nc.gpsimd.tensor_tensor(out_sb[:, n % 2, :, :], scaled[:, n % 2, :, :],
                                            x_sb[:, 2 * n:2 * n + 2, :], ALU.add).then_inc(out_ready, 1)

        @block.scalar
        def _(act):
            act.dma_start(ident_sb[:, :], ident).then_inc(ident_in, 16)
            for i, b in enumerate((bq, bk, bv)):
                act.dma_start(bias_bc[:, i * E:(i + 1) * E],
                              b.rearrange("(a n) -> a n", a=1).to_broadcast([P, E])).then_inc(bias_in, 16)
            act.dma_start(cos_sb[:, :, :], cos_t.rearrange("(t p) d -> p t d", p=P)).then_inc(rope_in, 16)
            act.dma_start(sin_sb[:, :, :], sin_t.rearrange("(t p) d -> p t d", p=P)).then_inc(rope_in, 16)
            act.dma_start(bo_bc[:, :], bo.rearrange("(a n) -> a n", a=1).to_broadcast([P, E])).then_inc(bo_in, 16)
            act.dma_start(down_bc[:, :], down_scale.rearrange("(a n) -> a n", a=1).to_broadcast([P, E])).then_inc(scale_in, 16)
            act.dma_start(gate_col[:, :], gate_scale.rearrange("(a p) -> p a", p=P),
                          allow_slow_non_contiguous=True).then_inc(scale_in, 16)
            act.dma_start(up_col[:, :], up_scale.rearrange("(a p) -> p a", p=P),
                          allow_slow_non_contiguous=True).then_inc(scale_in, 16)
            act.wait_ge(ident_in, 16)
            nc.scalar.copy(ident_bf[:, :], ident_sb[:, :]).then_inc(ident_ready, 1)
            for step in order["scalar"]:
                kind, n = step[:2]
                if kind == "w_copy":
                    act.wait_ge(w_turned, n + 1)
                    dst = w_t[:, :, n * E:(n + 1) * E] if n < 3 else wo_t[:, :, :]
                    nc.scalar.copy(dst, ps[:, banks_of["turn_w", n][0], :].rearrange("p (k f) -> p k f", k=EK)
                                   ).then_inc(w_copied, 1)
                elif kind == "xn_copy":
                    act.wait_ge(xn_turned, n + 1)
                    if n >= 4:
                        act.wait_ge(qkv_done, n - 3)
                    nc.scalar.copy(xn_t[:, n % 4, :, :],
                                   ps[:, banks_of["turn_xn", n][0], 0:EK * P].rearrange("p (k s) -> p k s", k=EK)
                                   ).then_inc(xn_copied, 1)
                elif kind == "p1":
                    act.wait_ge(rope_done, n + 1)
                    if n >= 2:
                        act.wait_ge(placed, n - 1)
                    nc.scalar.copy(part[0][:, n % 2, :], qk_rot[:, n % 2, :]).then_inc(p1_ready, 1)
                elif kind == "p2":
                    act.wait_ge(rest_ready, n + 1)
                    nc.scalar.copy(part[1][:, n % 2, :], rest[:, n % 2, :]).then_inc(p2_ready, 1)
                elif kind == "stack_act":
                    t, b = n // 3, n % 3 + 1
                    act.wait_ge(stack_turned, 4 * t + b + 1)
                    bank = banks_of["turn_stack", 4 * t + b][0]
                    nc.scalar.copy((q_stack, k_stack)[b // 2][0:STACK, 8 * (b % 2):8 * (b % 2) + 8, t * P:(t + 1) * P],
                                   ps[0:STACK, bank, :].bitcast(bf16).rearrange("p (h s) -> p h s", h=8)
                                   ).then_inc(stack_act, 1)
                elif kind == "exp":
                    u, m = step[1:]
                    j, pair, q0 = exps[u][m]
                    k = first_pv[u] + j
                    b0, b1 = banks_of["score", u, m]
                    act.wait_ge(scored, first_exp[u] + m + 1)
                    if k >= 2:
                        act.wait_ge(pv_done, k - 1)
                    nc.scalar.activation(probs[:, k % 2, 2 * pair:2 * pair + 2, q0:C],
                                         ps[:, b0:b1 + 1:b1 - b0, q0:C], ACT.Exp, scale=SCALE).then_inc(exp_done, 1)
                elif kind == "shift_copy":
                    act.wait_ge(shift_turned, n + 1)
                    if n >= 2:
                        act.wait_ge(shift_in[n - 2], 32)
                    nc.scalar.copy(max_rows[:, n % 2, :],
                                   ps[0:2 * G, banks_of["shift", n][0], 0:C // 2].bitcast(bf16)).then_inc(shift_copied, 1)
                elif kind == "o_copy":
                    act.wait_ge(pv_done, first_pv[n + 1])
                    if n >= 2:
                        act.wait_ge(o_turned, n - 1)
                    nc.scalar.copy(o_sb[:, n % 2, :], ps[:, banks_of["pv", n, 0][0], :]).then_inc(o_copied, 1)
                elif kind == "attn_copy":
                    act.wait_ge(attn_turned, n + 1)
                    if n >= 2:
                        act.wait_ge(projected, n - 1)
                    nc.scalar.copy(attn_t[:, n % 2, :, :],
                                   ps[:, banks_of["turn_attn", n][0], 0:EK * P].rearrange("p (k s) -> p k s", k=EK)
                                   ).then_inc(attn_copied, 1)
                elif kind == "xh":
                    c, i = divmod(n, TC)
                    act.wait_ge(xn2_turned, n + 1)
                    if c >= 1 and i == 0:
                        act.wait_ge(gu_done, FK * c)
                    nc.scalar.copy(xh[:, :, i * P:(i + 1) * P],
                                   ps[:, banks_of["turn_xn2", n][0], 0:EK * P].rearrange("p (k s) -> p k s", k=EK)
                                   ).then_inc(xh_ready, 1)
                elif kind == "tanh":
                    it = n % FK
                    act.wait_ge(gu_done, n + 1)
                    if n >= 2:
                        act.wait_ge(fuse_done, n - 1)
                    nc.scalar.activation(tanh_sb[:, n % 2, :], ps[:, banks_of["gate_up", n][0], :], ACT.Tanh,
                                         scale=half_gate[:, it:it + 1]).then_inc(tanh_done, 1)
                elif kind == "fh":
                    act.wait_ge(fuse_done, n + 1)
                    if n >= 2:
                        act.wait_ge(down_done, n - 1)
                    nc.scalar.copy(fh[:, n % 2, :], fuse[:, n % 2, :]).then_inc(fh_ready, 1)

        @block.vector
        def _(dve):
            n_steps = [0]

            def then_wait(ins):
                n_steps[0] += 1
                ins.then_inc(dve_step, 1)
                dve.wait_ge(dve_step, n_steps[0])

            nc.vector.memset(v_ones[:, :, :, D + 1:32], 0.0)
            nc.vector.memset(v_ones[:, :, :, D:D + 1], 1.0).then_inc(v_pads_set, 1)
            for step in order["vector"]:
                kind, n = step[:2]
                if kind == "stats":
                    dve.wait_ge(x_in[[t1 > n for _, t1 in X_LOADS].index(True)], 16)
                    i = n % 2
                    then_wait(nc.vector.bn_stats(stats[:, i, :], x_sb[:, n, :]))
                    then_wait(nc.vector.bn_aggr(mean_var[:, i, :], stats[:, i, :]))
                    nc.vector.tensor_scalar(var_eps[:, i, :], mean_var[:, i, 1:2], 1e-5, None, ALU.add).then_inc(var_ready, 1)
                elif kind == "xn":
                    dve.wait_ge(rstd_ready, n + 1)
                    if n >= 4:
                        dve.wait_ge(xn_turned, n - 3)
                    nc.vector.tensor_scalar(xn[:, n % 4, :], x_sb[:, n, :], mean_var[:, n % 2, 0:1], rstd[:, n % 2, :],
                                            ALU.subtract, ALU.mult).then_inc(xn_ready, 1)
                elif kind == "bias":
                    b0, b1 = banks_of["qkv", n]
                    if n == 0:
                        dve.wait_ge(bias_in, 48)
                    dve.wait_ge(qkv_done, n + 1)
                    if n >= 2:
                        dve.wait_ge(rope_mul, n - 1)
                    nc.vector.tensor_tensor(qk[:, n % 2, :], ps[:, b0, :], bias_bc[:, 0:2 * E], ALU.add).then_inc(qk_biased, 1)
                    nc.vector.tensor_tensor(v_ones[:, n, :, 0:D], ps[:, b1, 0:E].rearrange("p (h d) -> p h d", d=D),
                                            bias_bc[:, 2 * E:3 * E].rearrange("p (h d) -> p h d", d=D), ALU.add).then_inc(v_biased, 1)
                elif kind == "rope_sum":
                    dve.wait_ge(rope_mul, n + 1)
                    if n >= 2:
                        dve.wait_ge(rest_ready, n - 1)
                    nc.vector.tensor_tensor(qk_rot[:, n % 2, :], qk_cos[:, n % 2, :], qk_sin[:, n % 2, :],
                                            ALU.add).then_inc(rope_done, 1)
                elif kind == "rest":
                    dve.wait_ge(p1_ready, n + 1)
                    if n >= 2:
                        dve.wait_ge(p3_ready, n - 1)
                    nc.vector.tensor_tensor(rest[:, n % 2, :], qk_rot[:, n % 2, :], part[0][:, n % 2, :],
                                            ALU.subtract).then_inc(rest_ready, 1)
                elif kind == "place":
                    i = n % 2
                    dve.wait_ge(p3_ready, n + 1)
                    if n >= 2:
                        dve.wait_ge(stack_turned, 4 * (n - 1))
                    for side, slots in enumerate((Q_SLOTS, K_SLOTS)):
                        for p, (first, step_, count) in enumerate(slots):
                            dst = stacked[:, i, side * H:(side + 1) * H, first:first + step_ * (count - 1) + 1:step_, :]
                            src = part[p][:, i, side * E:(side + 1) * E].rearrange("p (h d) -> p h d", d=D)
                            last = nc.vector.tensor_copy(dst, src.unsqueeze(2).to_broadcast([P, H, count, D]))
                    last.then_inc(placed, 1)
                elif kind == "stack_dve":
                    dve.wait_ge(stack_turned, 4 * n + 1)
                    nc.vector.tensor_copy(q_stack[0:STACK, 0:8, n * P:(n + 1) * P],
                                          ps[0:STACK, banks_of["turn_stack", 4 * n][0], :].bitcast(bf16)
                                          .rearrange("p (h s) -> p h s", h=8)).then_inc(stack_dve, 1)
                elif kind == "exponent":
                    w = piece_width[n]
                    dve.wait_ge(raw_in[n % 2], 16 * (n // 2 + 1))
                    then_wait(nc.vector.tensor_scalar(w_exp[:, n % 2, 0:w].bitcast(i32), w_raw[:, n % 2, 0:w].bitcast(i32),
                                                      0x7F800000, None, ALU.bitwise_and))
                    nc.vector.tensor_scalar(w_exp[:, n % 2, 0:w], w_exp[:, n % 2, 0:w], 2.0 ** -6, 1.5 * 2.0 ** 20,
                                            ALU.max, ALU.mult).then_inc(exponent_ready, 1)
                elif kind == "check":
                    w = piece_width[n]
                    dve.wait_ge(piece_cut, 2 * (n + 1))
                    if n >= 1:
                        dve.wait_ge(piece_rounded, n)
                    nc.vector.tensor_scalar(w_chk[:, 0:w], w_raw[:, n % 2, 0:w], float(np.finfo(np.float32).max) / 464.0,
                                            0.0, ALU.mult, ALU.mult).then_inc(piece_checked, 1)
                elif kind == "taken":
                    u, m = step[1:]
                    h, t, k0, w, diagonal = pieces[u][m]
                    k = first_piece[u] + m
                    col = (t % TC) * G + h
                    bank = banks_of["max", u, m][0]
                    if k == 0:
                        dve.wait_ge(mask_in, 16)
                    dve.wait_ge(max_scored, k + 1)
                    if diagonal:
                        nc.vector.tensor_tensor_reduce(
                            out=max_junk[:, k % 2, 0:w], in0=ps[:, bank, 0:w], in1=causal_sb[:, C - w:C],
                            scale=1.0, scalar=-3.0e38, op0=ALU.add, op1=ALU.max,
                            accum_out=maxes[:, u % 2, k0 // C, col:col + 1]).then_inc(max_taken, 1)
                    else:
                        nc.vector.reduce_max(maxes[:, u % 2, k0 // C, col:col + 1], ps[:, bank, 0:w],
                                             AX.X).then_inc(max_taken, 1)
                elif kind == "neg":
                    c, i = units[n][0], n % 2
                    dve.wait_ge(max_taken, first_piece[n + 1])
                    top = maxes[:, i, 0, :]
                    if c >= 1:
                        then_wait(nc.vector.tensor_tensor(max_all[:, i, :], maxes[:, i, 0, :], maxes[:, i, 1, :], ALU.max))
                        top = max_all[:, i, :]
                    if n >= 2:
                        dve.wait_ge(shift_turned, n - 1)
                    top = top.rearrange("p (t h) -> p t h", h=G)
                    then_wait(nc.vector.tensor_scalar(neg_max[:, i, :, 0, :], top, -1.0, None, ALU.mult))
                    nc.vector.scalar_tensor_tensor(neg_max[:, i, :, 1, :], top, -1.0, neg_max[:, i, :, 0, :],
                                                   ALU.mult, ALU.subtract).then_inc(neg_ready, 1)
                elif kind == "norm":
                    c, g = units[n]
                    o = ps[:, banks_of["turn_o", n][0], :].rearrange("p (t h d) -> p t h d", h=G, d=32)
                    dve.wait_ge(o_turned, n + 1)
                    then_wait(nc.vector.reciprocal(inv_sum[:, n % 2, :, :], o[:, :, :, D]))
                    nc.vector.tensor_tensor(attn_s[:, TC * c:TC * (c + 1), g * G * D:(g + 1) * G * D]
                                            .rearrange("p t (h d) -> p t h d", d=D), o[:, :, :, 0:D],
                                            inv_sum[:, n % 2, :, :].unsqueeze(3).to_broadcast([P, TC, G, D]),
                                            ALU.mult).then_inc(normed, 1)
                elif kind == "resid":
                    dve.wait_ge(projected, n + 1)
                    dve.wait_ge(bo_added, n + 1)
                    nc.vector.tensor_tensor(x_sb[:, n, :], x_sb[:, n, :], ps[:, banks_of["project", n][0], 0:E],
                                            ALU.add).then_inc(resid_done, 1)
                elif kind == "stats2":
                    i = n % 2
                    dve.wait_ge(resid_done, n + 1)
                    then_wait(nc.vector.bn_stats(stats2[:, i, :], x_sb[:, n, :]))
                    then_wait(nc.vector.bn_aggr(mean_var2[:, i, :], stats2[:, i, :]))
                    nc.vector.tensor_scalar(var_eps2[:, i, :], mean_var2[:, i, 1:2], 1e-5, None, ALU.add).then_inc(var2_ready, 1)
                elif kind == "xn2":
                    dve.wait_ge(rstd2_ready, n + 1)
                    if n >= 2:
                        dve.wait_ge(xn2_turned, n - 1)
                    nc.vector.tensor_scalar(xn2[:, n % 2, :], x_sb[:, n, :], mean_var2[:, n % 2, 0:1], rstd2[:, n % 2, :],
                                            ALU.subtract, ALU.mult).then_inc(xn2_ready, 1)
                elif kind == "xl":
                    c, i = divmod(n, TC)
                    dve.wait_ge(xh_ready, n + 1)
                    nc.vector.tensor_tensor(xl[:, :, i * P:(i + 1) * P],
                                            ps[:, banks_of["turn_xn2", n][0], 0:EK * P].rearrange("p (k s) -> p k s", k=EK),
                                            xh[:, :, i * P:(i + 1) * P].bitcast(fp32), ALU.subtract).then_inc(xl_ready, 1)
                elif kind == "fuse":
                    it = n % FK
                    b0, b1 = banks_of["gate_up", n]
                    if n == 0:
                        then_wait(nc.vector.tensor_tensor(half_gu[:, :], half_gate[:, :], up_col[:, :], ALU.mult))
                    dve.wait_ge(tanh_done, n + 1)
                    then_wait(nc.vector.scalar_tensor_tensor(gated[:, n % 2, :], tanh_sb[:, n % 2, :], 1.0,
                                                             ps[:, b0, :], ALU.add, ALU.mult))
                    if n >= 2:
                        dve.wait_ge(fl_ready, n - 1)
                    nc.vector.scalar_tensor_tensor(fuse[:, n % 2, :], gated[:, n % 2, :], half_gu[:, it:it + 1],
                                                   ps[:, b1, :], ALU.mult, ALU.mult).then_inc(fuse_done, 1)
                elif kind == "scaled":
                    c, b = divmod(n, 2)
                    dve.wait_ge(down_done, FK * (c + 1))
                    if n >= 2:
                        dve.wait_ge(out_ready, n - 1)
                    nc.vector.tensor_tensor(scaled[:, b, :, :],
                                            ps[:, banks_of["down", FK * c][b], :].rearrange("p (t e) -> p t e", t=2),
                                            down_bc[:, :].unsqueeze(1).to_broadcast([P, 2, E]), ALU.mult).then_inc(scaled_done, 1)
                if step == ("bias", 0):
                    dve.wait_ge(scale_in, 48)
                    then_wait(nc.vector.tensor_scalar(half_gate[:, :], gate_col[:, :], 0.5, None, ALU.mult))

        @block.tensor
        def _(pe):
            empties = {"w_copy": w_copied, "xn_copy": xn_copied, "bias": v_biased, "stack_dve": stack_dve,
                       "stack_act": stack_act, "shift_copy": shift_copied, "o_copy": o_copied, "norm": normed,
                       "attn_copy": attn_copied, "resid": resid_done, "xl": xl_ready, "fuse": fuse_done,
                       "scaled": scaled_done}

            def emptied(step):
                if step[0] == "taken":
                    return max_taken, first_piece[step[1]] + step[2] + 1
                if step[0] == "exp":
                    return exp_done, first_exp[step[1]] + step[2] + 1
                return empties[step[0]], step[1] + 1

            for step in order["tensor"]:
                kind, n = step[:2]
                bank = banks_of.get(step, [None])
                for last_user in former.get(step, []):
                    if last_user:
                        pe.wait_ge(*emptied(last_user))
                if kind == "turn_w":
                    if n == 0:
                        pe.wait_ge(ident_in, 16)
                    pe.wait_ge(qkv_w_in[n] if n < 3 else wo_in, 16)
                    for k in range(EK):
                        for b in range(EK):
                            o = (k * EK + b) * P
                            last = nc.tensor.transpose(ps[:, bank[0], o:o + P], w_in[:, n, b, k * P:(k + 1) * P], ident_sb[:, :])
                    last.then_inc(w_turned, 1)
                elif kind == "turn_xn":
                    if n == 0:
                        pe.wait_ge(ident_in, 16)
                    pe.wait_ge(xn_ready, n + 1)
                    for k in range(EK):
                        last = nc.tensor.transpose(ps[:, bank[0], k * P:(k + 1) * P], xn[:, n % 4, k * P:(k + 1) * P], ident_sb[:, :])
                    last.then_inc(xn_turned, 1)
                elif kind == "qkv":
                    pe.wait_ge(xn_copied, n + 1)
                    if n == 0:
                        pe.wait_ge(w_copied, 3)
                    for o, f0, f1 in ((bank[0], 0, 2 * E), (bank[1], 2 * E, 3 * E)):
                        for k in range(EK):
                            last = nc.tensor.matmul(ps[:, o, 0:f1 - f0], xn_t[:, n % 4, k, :], w_t[:, k, f0:f1],
                                                    start=(k == 0), stop=(k == EK - 1))
                    last.then_inc(qkv_done, 1)
                elif kind == "turn_stack":
                    t, b = divmod(n, 4)
                    if n == 0:
                        pe.wait_ge(ident_ready, 1)
                    pe.wait_ge(placed, t + 1)
                    o = ps[0:STACK, bank[0], :].bitcast(bf16)
                    for h in range(8):
                        last = nc.tensor.transpose(o[:, h * P:(h + 1) * P],
                                                   stacked[:, t % 2, 8 * b + h, :, :].rearrange("p b d -> p (b d)"),
                                                   ident_bf[:, :])
                    last.then_inc(stack_turned, 1)
                elif kind == "max":
                    u, m = step[1:]
                    c, g = units[u]
                    h, t, k0, w, _ = pieces[u][m]
                    if m == 0:
                        pe.wait_ge(stack_dve, TC * (c + 1))
                        pe.wait_ge(stack_act, 3 * TC * (c + 1))
                    if first_piece[u] + m >= 2:
                        pe.wait_ge(max_taken, first_piece[u] + m - 1)
                    nc.tensor.matmul(ps[:, bank[0], 0:w], q_stack[0:STACK, g * G + h, t * P:(t + 1) * P],
                                     k_stack[0:STACK, g * G + h, k0:k0 + w], start=True, stop=True).then_inc(max_scored, 1)
                elif kind == "shift":
                    pe.wait_ge(neg_ready, n + 1)
                    for i in range(TC):
                        last = nc.tensor.transpose(ps[0:2 * G, bank[0], i * P // 2:(i + 1) * P // 2].bitcast(bf16),
                                                   neg_max[:, n % 2, i, :, :].rearrange("p a h -> p (a h)"), ident_bf[:, :])
                    last.then_inc(shift_turned, 1)
                elif kind == "score":
                    u, m = step[1:]
                    c, g = units[u]
                    j, pair, q0 = exps[u][m]
                    if m == 0:
                        if u == 0:
                            pe.wait_ge(ones_in, 16)
                            pe.wait_ge(stack_dve, T)
                            pe.wait_ge(stack_act, 3 * T)
                        pe.wait_ge(shift_in[u], 32)
                    for i in range(2):
                        h = g * G + 2 * pair + i
                        last = nc.tensor.matmul(ps[:, bank[i], q0:C], k_stack[0:ROWS, h, j * P:(j + 1) * P],
                                                q_stack[0:ROWS, h, c * C + q0:(c + 1) * C], start=True, stop=True)
                    last.then_inc(scored, 1)
                elif kind == "pv":
                    u, j = step[1:]
                    c, g = units[u]
                    k = first_pv[u] + j
                    q0 = max(0, (j - TC * c) * P)
                    o = banks_of["pv", u, 0][0]
                    if k == 0:
                        pe.wait_ge(v_biased, T)
                        pe.wait_ge(v_pads_set, 1)
                    pe.wait_ge(exp_done, 2 * (k + 1))
                    if j >= TC * c:
                        pe.wait_ge(masked, TC * u + j - TC * c + 1)
                    for h in range(G):
                        last = nc.tensor.matmul(ps[32 * h:32 * h + 32, o, q0:C], v_ones[:, j, g * G + h, :],
                                                probs[:, k % 2, h, q0:C], start=(j == 0), stop=(j == TC * (c + 1) - 1))
                    last.then_inc(pv_done, 1)
                elif kind == "turn_o":
                    pe.wait_ge(o_copied, n + 1)
                    for i in range(TC):
                        last = nc.tensor.transpose(ps[:, bank[0], i * P:(i + 1) * P], o_sb[:, n % 2, i * P:(i + 1) * P], ident_sb[:, :])
                    last.then_inc(o_turned, 1)
                elif kind == "turn_attn":
                    pe.wait_ge(normed, NG * (n // TC + 1))
                    for k in range(EK):
                        last = nc.tensor.transpose(ps[:, bank[0], k * P:(k + 1) * P], attn_s[:, n, k * P:(k + 1) * P], ident_sb[:, :])
                    last.then_inc(attn_turned, 1)
                elif kind == "project":
                    pe.wait_ge(attn_copied, n + 1)
                    if n == 0:
                        pe.wait_ge(w_copied, 4)
                    for k in range(EK):
                        last = nc.tensor.matmul(ps[:, bank[0], 0:E], attn_t[:, n % 2, k, :], wo_t[:, k, :],
                                                start=(k == 0), stop=(k == EK - 1))
                    last.then_inc(projected, 1)
                elif kind == "turn_xn2":
                    pe.wait_ge(xn2_ready, n + 1)
                    for k in range(EK):
                        last = nc.tensor.transpose(ps[:, bank[0], k * P:(k + 1) * P], xn2[:, n % 2, k * P:(k + 1) * P], ident_sb[:, :])
                    last.then_inc(xn2_turned, 1)
                elif kind == "gate_up":
                    c, it = divmod(n, FK)
                    if it == 0:
                        pe.wait_ge(xh_ready, TC * (c + 1))
                        pe.wait_ge(xl_ready, TC * (c + 1))
                    if n == 0:
                        pe.wait_ge(piece_rounded, len(weight_pieces))
                    if n >= 2:
                        pe.wait_ge(fuse_done, n - 1)
                    for o, w in ((bank[0], w_gate), (bank[1], w_up)):
                        for k in range(EK):
                            for a, xs in enumerate((xh, xl)):
                                last = nc.tensor.matmul(ps[:, o, :], w[:, k, it * P:(it + 1) * P], xs[:, k, :],
                                                        start=(k == 0 and a == 0), stop=(k == EK - 1 and a == 1))
                    last.then_inc(gu_done, 1)
                elif kind == "down":
                    c, it = divmod(n, FK)
                    o = banks_of["down", FK * c]
                    pe.wait_ge(fh_ready, n + 1)
                    pe.wait_ge(fl_ready, n + 1)
                    for i in range(TC):
                        for a, fs in enumerate((fh, fl)):
                            last = nc.tensor.matmul(ps[:, o[i // 2], (i % 2) * E:(i % 2 + 1) * E],
                                                    fs[:, n % 2, i * P:(i + 1) * P], w_down[:, it, :],
                                                    start=(it == 0 and a == 0 and i % 2 == 0),
                                                    stop=(it == FK - 1 and a == 1), skip_group_check=True)
                    last.then_inc(down_done, 1)


_INS = ['L0_attn_x', 'L0_attn_Wq', 'L0_attn_bq', 'L0_attn_Wk', 'L0_attn_bk', 'L0_attn_Wv', 'L0_attn_bv',
        'L0_attn_Wo', 'L0_attn_bo', 'L0_ffn_gate_w', 'L0_ffn_up_w', 'L0_ffn_down_w', 'L0_ffn_gate_scale',
        'L0_ffn_up_scale', 'L0_ffn_down_scale']


def _constants():
    S, D, C = 1024, 16, 512
    pos = np.arange(S, dtype=np.float32)[:, None]
    theta = np.repeat(-np.arange(0, D, 2, dtype=np.float32) / np.float32(D), 2)
    angles = pos * np.power(np.float32(10000.0), theta)[None, :]
    sign = np.where(np.arange(D) % 2 == 0, -1.0, 1.0).astype(np.float32)
    causal = np.zeros((P, C), np.float32)
    causal[:, C - P:] = np.where(np.arange(P)[None, :] > np.arange(P)[:, None], -3.0e38, 0.0)
    return {"cos": np.cos(angles), "sin": np.sin(angles) * sign, "causal": causal,
            "ident": np.eye(P, dtype=np.float32)}


def kernel(**inputs):
    import concourse.bacc as _bacc
    from concourse.bass_utils import run_bass_kernel_spmd as _run

    nc = _bacc.Bacc("TRN2", target_bir_lowering=False, num_devices=1)
    arrays, args = {}, []
    for name, a in [(n, inputs[n]) for n in _INS] + list(_constants().items()):
        a = np.ascontiguousarray(a)
        arrays[f"in_{name}_dram"] = a
        args.append(nc.dram_tensor(f"in_{name}_dram", a.shape, mybir.dt.from_np(a.dtype), kind="ExternalInput").ap())
    out = nc.dram_tensor("out_0_dram", (1, 1024, 256), mybir.dt.float32, kind="ExternalOutput").ap()
    build(nc, *args, out)
    r = _run(nc, [arrays], core_ids=[0])
    return r.results[0]["out_0_dram"]
```

```python
import numpy as np
import concourse.bass as bass
from concourse import mybir
from concourse.alu_op_type import AluOpType as ALU
from contextlib import ExitStack

P = 128


PATIENCE = {
    'gpsimd': 400, 'scalar': 100, 'tensor': 100,
}
FAVOUR = {
    'attn_copy': (-5000, 1000), 'bias': (-20000, -20000), 'bias_v': (-10000, -10000),
    'bo': (-1000, -80000), 'check': (-40000, -40000), 'eps': (-5000, 10000), 'eps2': (3000, 0),
    'exp': (20000, 1000), 'exponent': (-3000, 1000), 'fh': (-1000, 0), 'fl': (0, 300),
    'fuse': (-40000, 0), 'gated': (80000, 80000), 'magic': (20000, 20000), 'mask': (-40000, 0),
    'max': (-10000, -3000), 'mean': (300, -3000), 'mean2': (20000, 1000), 'neg': (20000, 20000),
    'norm': (10000, 10000), 'o_copy': (-10000, 20000), 'out': (-20000, -20000),
    'p1': (-300, -10000), 'p2': (300, 80000), 'p3': (5000, -40000), 'power': (0, -300),
    'power2': (0, 10000), 'project': (1000, 1000), 'pv': (300, 300), 'resid': (5000, 10000),
    'rest': (10000, 10000), 'rope': (300, 300), 'rope_cos': (-5000, 300),
    'rope_sum': (-10000, 20000), 'round': (-40000, -40000), 'rounded': (1000, 3000),
    'scaled': (-40000, 3000), 'shift': (20000, -1000), 'shift_copy': (-1000, -10000),
    'spread': (3000, 3000), 'stack_act': (-20000, -40000), 'stack_dve': (80000, 0),
    'stats': (3000, -20000), 'taken': (-40000, -40000), 'tanh': (-3000, -3000),
    'turn_attn': (300, 300), 'turn_o': (-1000, 300), 'turn_stack': (-10000, -10000),
    'turn_w': (-3000, 3000), 'turn_xn2': (10000, 1000), 'up': (-300, 40000), 'v': (-300, -1000),
    'w_copy': (-5000, -3000), 'xh': (-5000, -5000), 'xl': (3000, -20000), 'xn': (-1000, -1000),
    'xn2': (10000, 3000), 'xn_copy': (10000, 0),
}


STACKS_BY_DVE = [1, 4, 8, 15, 20, 25]
COS_BY_DVE = [0, 2, 3, 6]
SPREAD_BY_DVE = [0, 3, 6]
WARM_UP = {("turn_w", 0): 8, ("turn_xn", 1): 3, ("qk", 0): 2}
FAR = [(4, 4, 1), (4, 5, 1), (6, 7, 1), (7, 6, 1)]
MAX_AHEAD = 3
ROUND_AT = 60000.0
SECOND_PASS = [0, 1, 2, 3, 4, 5, 6, 7]


class Plan:

    HOP, HOP_TO_PE = 200.0, 290.0
    HOP_SAME = 80.0

    def __init__(self, patience, favour):
        self.steps, self.last = {}, {}
        self.patience, self.favour = patience, favour

    def add(self, step, engine, ns, after=(), banks=0, keeps=False, frees=None, late=0.0):
        kind = step[0]
        after = [a for a in after if a is not None]
        if kind in self.last:
            after.append(self.last[kind])
        self.steps[step] = (engine, ns, after, banks, frees, late)
        self.last[kind] = step

    @staticmethod
    def choose(bank_free, banks, t):
        if banks == 2:
            pairs = [(max(t, bank_free[b][0], bank_free[b + 1][0]), b) for b in range(0, 8, 2)
                     if b in bank_free and b + 1 in bank_free]
            return [min(pairs)[1], min(pairs)[1] + 1] if pairs else None
        singles = [(max(t, bank_free[b][0]), b ^ 1 in bank_free, b) for b in bank_free]
        return [min(singles)[2]] if singles else None

    def solve(self):
        steps = self.steps
        behind, users = {}, {k: [] for k in steps}
        for k, (_, _, after, _, _, _) in steps.items():
            for a in after:
                users[a].append(k)
        todo = {k: len(v[2]) for k, v in steps.items()}
        topo = [k for k in steps if not todo[k]]
        for k in topo:
            for u in users[k]:
                todo[u] -= 1
                if not todo[u]:
                    topo.append(u)
        assert len(topo) == len(steps), "a circle of steps"
        for k in reversed(topo):
            behind[k] = steps[k][1] + steps[k][5] + max([behind[u] for u in users[k]], default=0.0)
        todo = {k: len(v[2]) for k, v in steps.items()}
        place = {k: i for i, k in enumerate(steps)}
        kinds, seen = {}, {}
        for k in steps:
            kinds[k[0]] = kinds.get(k[0], 0) + 1
        urgency = {}
        for k in steps:
            n = seen[k[0]] = seen.get(k[0], 0) + 1
            urgency[k] = behind[k] + self.favour.get(k[0], (0, 0))[2 * n > kinds[k[0]]]
        end, free_at, inputs_at = {}, {}, {}
        ready = set()

        def add_ready(k):
            engine, _, after, _, _, _ = steps[k]
            t = 0.0
            for a in after:
                if steps[a][0] != engine:
                    hop = self.HOP_TO_PE if engine == "tensor" else self.HOP
                else:
                    hop = 0.0 if a[0] == k[0] or engine == "tensor" else self.HOP_SAME
                t = max(t, end[a] + hop)
            inputs_at[k] = t
            ready.add(k)

        for k in steps:
            if not todo[k]:
                add_ready(k)
        bank_free = {b: (0.0, None) for b in range(8)}
        held = {}
        order, banks_of, former = {}, {}, {}
        while ready:
            starts = {}
            for k in ready:
                engine, banks = steps[k][0], steps[k][3]
                t = max(free_at.get(engine, 0.0), inputs_at[k])
                if banks:
                    mine = self.choose(bank_free, banks, t)
                    if mine is None:
                        continue
                    t = max(t, max(bank_free[b][0] for b in mine))
                starts[k] = t
            assert starts, "no step can start"
            first = min(starts, key=lambda k: (starts[k], place[k]))
            engine = steps[first][0]
            latest = starts[first] + self.patience.get(engine, 0.0)
            rivals = [k for k in starts if steps[k][0] == engine and starts[k] <= latest]
            k = max(rivals, key=lambda k: (urgency[k], -starts[k], -place[k]))
            t = starts[k]
            engine, ns, after, banks, frees, late = steps[k]
            ready.discard(k)
            if banks:
                mine = self.choose(bank_free, banks, t)
                former[k] = [bank_free.pop(b)[1] for b in mine]
                banks_of[k] = held[k] = mine
            order.setdefault(engine, []).append(k)
            free_at[engine] = t + ns
            end[k] = t + ns + late
            if frees is not None:
                for b in held.pop(frees):
                    bank_free[b] = (end[k] + self.HOP, k)
            for u in users[k]:
                todo[u] -= 1
                if not todo[u]:
                    add_ready(u)
        return order, banks_of, former, max(end.values())


class Work:

    def __init__(self, T, TC, NG, G, C):
        self.units = units = [(c, g) for c in range(T // TC) for g in range(NG)]
        self.second = [units[u] for u in SECOND_PASS]
        self.pieces = [[] for _ in units]
        self.far = [[] for _ in units]
        for u, (c, g) in enumerate(units):
            for t in range(TC * c, TC * c + TC):
                self.far[u] += [(t, pair) for pair in range(G // 2) if c and (u, t, pair) in FAR]
                for h in range(G):
                    for k0 in range(0, (t + 1) * P, C):
                        w = min(C, (t + 1) * P - k0)
                        if k0 or (t, h // 2) not in self.far[u]:
                            self.pieces[u].append((h, t, k0, w, k0 + w == (t + 1) * P))
        self.exps = [[(j, pair, max(0, (j - TC * c) * P)) for j in range(TC * (c + 1)) for pair in range(2)]
                     for c, g in self.second]
        n = range(len(units) + 1)
        self.first_piece = [sum(len(p) for p in self.pieces[:u]) for u in n]
        self.first_far = [sum(len(f) for f in self.far[:u]) for u in n]
        self.first_exp = [sum(len(e) for e in self.exps[:u]) for u in n]
        self.first_pv = [e // 2 for e in self.first_exp]


def plan_steps(T, TC, NG, FK, C, work, weight_pieces):
    p = Plan(PATIENCE, FAVOUR)
    units, pieces, far, exps = work.units, work.pieces, work.far, work.exps
    first_piece, first_far, first_exp, first_pv = work.first_piece, work.first_far, work.first_exp, work.first_pv
    NC = T // TC

    def at(kind, n):
        return (kind, n) if n >= 0 else None

    def by_stack(n):
        return ("stack_dve" if n in STACKS_BY_DVE else "stack_act", n)

    all_stacks = [by_stack(n) for n in range(4 * T)]

    arrivals = {"x_in": [2700, 4200, 5700, 7200] + [8700] * 4, "w_in": [4300, 5800, 7300, 8800],
                "bias_in": [6100, 7200], "rope_in": [8100], "bo_in": [10700]}
    for kind, times in arrivals.items():
        for n, ns in enumerate(times):
            p.add((kind, n), f"dma_{kind}{n}", float(ns))
    for i in range(3):
        p.add(("turn_w", i), "tensor", 700.0, [("w_in", i)], banks=1)
        p.add(("w_copy", i), "scalar", 478.0, [("turn_w", i)], frees=("turn_w", i))
    p.add(("turn_w", 3), "tensor", 430.0, [("w_in", 3)], banks=1)
    p.add(("w_copy", 3), "scalar", 478.0, [("turn_w", 3), ("w_copy", 2)], frees=("turn_w", 3))
    for t in range(T):
        p.add(("stats", t), "vector", 335.0, [("x_in", t), at("mean", t - 2)])
        p.add(("mean", t), "vector", 80.0, [("stats", t), at("xn", t - 2)])
        p.add(("eps", t), "vector", 65.0, [("mean", t)])
        p.add(("power", t), "gpsimd", 464.0, [("eps", t)])
        p.add(("xn", t), "vector", 323.0, [("power", t), at("turn_xn", t - 2)])
        p.add(("bo", t), "gpsimd", 687.0, [("xn", t), ("bo_in", 0)])
        p.add(("turn_xn", t), "tensor", 220.0, [("xn", t)], banks=1)
        p.add(("xn_copy", t), "scalar", 264.0, [("turn_xn", t), at("v", t - 4)], frees=("turn_xn", t))
        p.add(("qk", t), "tensor", 1710.0, [("xn_copy", t), ("w_copy", 1)], banks=1)
        p.add(("bias", t), "vector", 600.0, [("qk", t), at("rope", t - 2), ("bias_in", 0)], frees=("qk", t))
        p.add(("v", t), "tensor", 860.0, [("qk", t), ("w_copy", 2)], banks=1)
        p.add(("bias_v", t), "vector", 335.0, [("v", t), ("bias_in", 1)], frees=("v", t))
        cos_dve = t in COS_BY_DVE
        if cos_dve:
            p.add(("rope_cos", t), "vector", 600.0, [("bias", t), ("rope_in", 0), at("rope_sum", t - 2)])
        p.add(("rope", t), "gpsimd", 1700.0 if cos_dve else 2830.0, [("bias", t), ("rope_in", 0), at("rope_sum", t - 2)])
        p.add(("rope_sum", t), "vector", 600.0, [("rope", t), ("rope_cos", t) if cos_dve else None, at("rest", t - 2)])
        spread = t in SPREAD_BY_DVE
        p.add(("p1", t), "scalar", 530.0 if spread else 1380.0, [("rope_sum", t), at("turn_stack", 4 * (t - 2) + 3)])
        p.add(("rest", t), "vector", 660.0, [("p1", t), at("p3", t - 2)])
        if spread:
            p.add(("spread", t), "vector", 400.0, [("p1", t)])
        p.add(("p2", t), "scalar", 960.0, [("rest", t)])
        p.add(("p3", t), "gpsimd", 1200.0, [("p2", t)])
        for b in range(4):
            n = 4 * t + b
            p.add(("turn_stack", n), "tensor", 450.0, [("p3", t), ("spread", t) if spread else None, at("turn_stack", n - 1)], banks=1)
            if n in STACKS_BY_DVE:
                p.add(("stack_dve", n), "vector", 600.0, [("turn_stack", n)], frees=("turn_stack", n))
            else:
                p.add(("stack_act", n), "scalar", 904.0, [("turn_stack", n)], frees=("turn_stack", n))
    N = len(weight_pieces)
    p.add(("rounding_begins", 0), "clock", ROUND_AT)
    for n in range(N):
        p.add(("raw", n), "sync", 100.0, [at("rounded", n - 2), ("rounding_begins", 0)], late=2500.0)
        p.add(("exponent", n), "vector", 240.0, [("raw", n), at("round", n - 2)])
        p.add(("magic", n), "vector", 240.0, [("exponent", n)])
        p.add(("round", n), "gpsimd", 1780.0, [("magic", n)])
        p.add(("check", n), "vector", 240.0, [("round", n), at("rounded", n - 1)])
        p.add(("rounded", n), "gpsimd", 841.0, [("check", n)])
    for u, (c, g) in enumerate(units):
        stacks = [by_stack(n) for n in range(4 * TC * (c + 1))]
        for m, (_, t, _, w, _) in enumerate(pieces[u]):
            n = first_piece[u] + m
            p.add(("max", u, m), "tensor", w / 2.4 + 3.0,
                  [*stacks[:4 * (t + 1)], flat(pieces, first_piece, n - 1, "max"),
                   flat(pieces, first_piece, n - MAX_AHEAD, "taken")], banks=1)
            p.add(("taken", u, m), "vector", w / 0.96 + 70.0, [("max", u, m), at("neg", u - 2)], frees=("max", u, m))
        for n in range(first_far[u], first_far[u + 1]):
            p.add(("far", n), "tensor", 430.0, stacks, banks=2)
            p.add(("far_taken", n), "vector", 1132.0, [("far", n), at("neg", u - 2)], frees=("far", n))
        p.add(("neg", u), "vector", 520.0, [("taken", u, len(pieces[u]) - 1), at("far_taken", first_far[u + 1] - 1),
                                            at("shift", u - 2)])
        p.add(("shift", u), "tensor", 150.0, [("neg", u)], banks=1)
        p.add(("shift_copy", u), "scalar", 478.0, [("shift", u), at("shift_in", u - 2)], frees=("shift", u))
        p.add(("shift_in", u), "sync", 200.0, [("shift_copy", u)], late=2300.0)
    for v, u in enumerate(SECOND_PASS):
        c, g = units[u]
        for m, (j, pair, q0) in enumerate(exps[v]):
            e, n = first_exp[v] + m, first_pv[v] + j
            p.add(("score", v, m), "tensor", 2 * (C - q0) / 2.4 + 6.0,
                  [("shift_in", u), flat(exps, first_exp, e - 1, "score"),
                   flat(exps, first_exp, e - 2, "exp")], banks=2)
            p.add(("exp", v, m), "scalar", 2 * (C - q0) / 1.2 + 51.0,
                  [("score", v, m), flat([e[::2] for e in exps], first_pv, n - 2, "pv")], frees=("score", v, m))
            if pair == 1:
                if j >= TC * c:
                    p.add(("mask", v, j), "gpsimd", 600.0, [("exp", v, m)])
                p.add(("pv", v, j), "tensor", 940.0 * (C - q0) / C,
                      [("exp", v, m), ("mask", v, j) if j >= TC * c else None,
                       ("bias_v", TC * (c + 1) - 1), ("o_copy", v - 1) if v and j == 0 else None],
                      banks=1 if j == 0 else 0)
        p.add(("o_copy", v), "scalar", 478.0, [("pv", v, exps[v][-1][0]), at("turn_o", v - 2)], frees=("pv", v, 0))
        p.add(("turn_o", v), "tensor", 440.0, [("o_copy", v), ("turn_w", 3)], banks=1)
        p.add(("norm", v), "vector", 630.0, [("turn_o", v), at("norm", v - 1)], frees=("turn_o", v))
    for t in range(T):
        c = t // TC
        p.add(("turn_attn", t), "tensor", 220.0, [("norm", chunk_done(units, c) - 1), *all_stacks], banks=1)
        p.add(("attn_copy", t), "scalar", 264.0, [("turn_attn", t), at("project", t - 2)], frees=("turn_attn", t))
        p.add(("project", t), "tensor", 880.0, [("attn_copy", t), ("w_copy", 3)], banks=1)
        p.add(("resid", t), "vector", 335.0, [("project", t), ("bo", T - 1)], frees=("project", t))
        p.add(("stats2", t), "vector", 335.0, [("resid", t), at("mean2", t - 2)])
        p.add(("mean2", t), "vector", 80.0, [("stats2", t), at("xn2", t - 2)])
        p.add(("eps2", t), "vector", 65.0, [("mean2", t)])
        p.add(("power2", t), "gpsimd", 464.0, [("eps2", t)])
        p.add(("xn2", t), "vector", 323.0, [("power2", t), at("turn_xn2", t - 2)])
        p.add(("turn_xn2", t), "tensor", 220.0, [("xn2", t)], banks=1)
        free = [("up", FK * c - 1)] if c else []
        p.add(("xh", t), "scalar", 264.0, [("turn_xn2", t)] + free)
        p.add(("xl", t), "vector", 335.0, [("xh", t)], frees=("turn_xn2", t))
    for n in range(FK * NC):
        c, it = divmod(n, FK)
        p.add(("gate", n), "tensor", 860.0, [("xl", TC * (c + 1) - 1), ("rounded", N - 1)], banks=1)
        p.add(("tanh", n), "scalar", 571.0, [("gate", n), at("gated", n - 2)])
        p.add(("gated", n), "vector", 600.0, [("tanh", n), at("fuse", n - 2)], frees=("gate", n))
        p.add(("up", n), "tensor", 860.0, [("gate", n)], banks=1)
        p.add(("fuse", n), "vector", 600.0, [("up", n), ("gated", n), at("fl", n - 2)], frees=("up", n))
        p.add(("fh", n), "scalar", 520.0, [("fuse", n), at("down", n - 2)])
        p.add(("fl", n), "gpsimd", 1225.0, [("fh", n)])
        p.add(("down", n), "tensor", 900.0, [("fl", n), at("scaled", 2 * c - 1) if it == 0 else None],
              banks=2 if it == 0 else 0)
    for c in range(NC):
        for b in range(2):
            k = 2 * c + b
            p.add(("scaled", k), "vector", 600.0, [("down", FK * (c + 1) - 1), at("out", k - 2)],
                  frees=("down", FK * c) if b else None)
            p.add(("out", k), "gpsimd", 1225.0, [("scaled", k), at("store", k - 2)])
            p.add(("store", k), "sync", 100.0, [("out", k)], late=2300.0)
    return p.solve()


def chunk_done(units, c):
    return max(v for v, u in enumerate(SECOND_PASS) if units[u][0] == c) + 1


def flat(lists, first, n, kind):
    if n < 0:
        return None
    u = max(i for i in range(len(lists)) if first[i] <= n)
    if kind == "pv":
        return (kind, u, n - first[u])
    return (kind, u, n - first[u])


def build(nc, x, Wq, bq, Wk, bk, Wv, bv, Wo, bo, gate_w, up_w, down_w, gate_scale, up_scale,
          down_scale, cos_t, sin_t, causal, ident, out):
    fp32, bf16, fp32r, i32 = mybir.dt.float32, mybir.dt.bfloat16, mybir.dt.float32r, mybir.dt.int32
    ACT = mybir.ActivationFunctionType
    AX = mybir.AxisListType

    S, E = x.shape[1], x.shape[2]
    H, D = 16, 16
    F = gate_w.shape[1]
    T = S // P
    EK = E // P
    FK = F // P
    C = 512
    NC = S // C
    TC = C // P
    G = 4
    NG = H // G
    SCALE = 1.0 / float(np.sqrt(D))
    STACK = 6 * D
    ROWS = STACK + 2

    X_LOADS = [(0, 1), (1, 2), (2, 4), (4, T)]
    P1_BLOCKS = (slice(0, 3), slice(1, 6, 2))
    P2_BLOCKS = (slice(3, 5), slice(0, 5, 4))
    P3_BLOCKS = (slice(5, 6), slice(2, 3))
    P1_FIRST, P1_OTHERS = (slice(0, 1), slice(1, 2)), (slice(1, 3), slice(3, 6, 2))
    P2_FIRST = (slice(3, 4), slice(0, 1))

    work = Work(T, TC, NG, G, C)
    units, second, pieces, far, exps = work.units, work.second, work.pieces, work.far, work.exps
    first_piece, first_far, first_exp, first_pv = work.first_piece, work.first_far, work.first_exp, work.first_pv

    WP = 384
    weight_pieces = []
    for m in range(2):
        weight_pieces += [(m, kt, c0) for kt in range(EK) for c0 in range(0, F, WP)]
    weight_pieces += [(2, kt, 0) for kt in range(0, FK)]

    order, banks_of, former, _ = plan_steps(T, TC, NG, FK, C, work, weight_pieces)

    ctx = ExitStack()
    with ctx:
        def sb(name, shape, dt=fp32, scope=ctx):
            return scope.enter_context(nc.sbuf_tensor(name, shape, dt))

        def sem(name):
            return ctx.enter_context(nc.semaphore(name))

        x_sb = sb("x_sb", [P, T, E])
        q_stack = sb("q_stack", [P, H, S], bf16)
        k_stack = sb("k_stack", [P, H, S], bf16)
        v_ones = sb("v_ones", [P, T, H, 32])
        probs = sb("probs", [P, 2, G, C])
        wo_t = sb("wo_t", [P, EK, E])
        w_gate = sb("w_gate", [P, EK, F], fp32r)
        w_up = sb("w_up", [P, EK, F], fp32r)
        w_down = sb("w_down", [P, FK, E], fp32r)
        causal_sb = sb("causal_sb", [P, C])
        ident_sb = sb("ident_sb", [P, P])
        ident_bf = sb("ident_bf", [P, P], bf16)
        warm = sb("warm", [P, C], bf16)
        exp_of_zero = sb("exp_of_zero", [1, 1])
        ones_row = sb("ones_row", [2, S], bf16)
        bo_bc = sb("bo_bc", [P, E])
        down_bc = sb("down_bc", [P, E])
        gate_col = sb("gate_col", [P, FK])
        up_col = sb("up_col", [P, FK])
        half_gate = sb("half_gate", [P, FK])
        half_gu = sb("half_gu", [P, FK])
        w_raw = sb("w_raw", [P, 2, WP])
        w_exp = sb("w_exp", [P, 2, WP])
        w_chk = sb("w_chk", [P, WP])
        maxes = sb("maxes", [P, 2, 2, G * TC])
        max_all = sb("max_all", [P, 2, G * TC])
        neg_max = sb("neg_max", [P, 2, TC, 2, G], bf16)
        max_rows = sb("max_rows", [2 * G, 2, C], bf16)
        max_junk = sb("max_junk", [P, 4, C], bf16)
        stats = sb("stats", [P, 2, 6])
        mean_var = sb("mean_var", [P, 2, 2])
        var_eps = sb("var_eps", [P, 2, 1])
        rstd = sb("rstd", [P, 2, 1])
        stats2 = sb("stats2", [P, 2, 6])
        mean_var2 = sb("mean_var2", [P, 2, 2])
        var_eps2 = sb("var_eps2", [P, 2, 1])
        rstd2 = sb("rstd2", [P, 2, 1])
        minus_half = sb("minus_half", [P, 1])
        inv_sum = sb("inv_sum", [P, 2, TC, G])

        loaded = ExitStack()
        w_in = sb("w_in", [P, 4, EK, E], scope=loaded)
        loaded.close()
        attn_s = sb("attn_s", [P, T, E])
        o_sb = sb("o_sb", [P, 2, C])

        early = ExitStack()

        def sa(name, shape, dt=fp32):
            return sb(name, shape, dt, early)
        w_t = sa("w_t", [P, EK, 3 * E])
        bias_bc = sa("bias_bc", [P, 3 * E])
        cos_sb = sa("cos_sb", [P, T, D])
        sin_sb = sa("sin_sb", [P, T, D])
        xn = sa("xn", [P, 2, E])
        xn_t = sa("xn_t", [P, 4, EK, P])
        qk = sa("qk", [P, 2, 2 * E])
        qk_cos = sa("qk_cos", [P, 2, 2 * E])
        qk_sin = sa("qk_sin", [P, 2, 2 * E])
        qk_rot = sa("qk_rot", [P, 2, 2 * E])
        rest = sa("rest", [P, 2, 2 * E])
        parts = sa("parts", [P, 2, 2 * H, 6, D], bf16)
        early.close()
        attn_t = sb("attn_t", [P, 2, EK, P])
        xn2 = sb("xn2", [P, 2, E])
        xh = sb("xh", [P, EK, C], fp32r)
        xl = sb("xl", [P, EK, C], fp32r)
        tanh_sb = sb("tanh_sb", [P, 2, C])
        gated = sb("gated", [P, 2, C])
        fuse = sb("fuse", [P, 2, C])
        fh = sb("fh", [P, 2, C], fp32r)
        fl = sb("fl", [P, 2, C], fp32r)
        scaled = sb("scaled", [P, 2, 2, E])
        out_sb = sb("out_sb", [P, 2, 2, E])

        ps = ctx.enter_context(nc.psum_tensor("ps", [P, 8, C], fp32))

        x_in = [sem(f"x_in{n}") for n in range(len(X_LOADS))]
        qkv_w_in = [sem(f"qkv_w_in{i}") for i in range(3)]
        wo_in, bias_in, rope_in = sem("wo_in"), sem("bias_in"), sem("rope_in")
        ident_in, mask_in, scale_in, bo_in, ones_in = (sem("ident_in"), sem("mask_in"), sem("scale_in"),
                                                       sem("bo_in"), sem("ones_in"))
        raw_in = [sem(f"raw_in{i}") for i in range(2)]
        shift_in = [sem(f"shift_in{u}") for u in range(len(units))]
        stored = [sem(f"stored{k}") for k in range(2 * NC)]
        warm_set = sem("warm_set")
        half_set, ones_set, v_pads_set, ident_ready = (sem("half_set"), sem("ones_set"), sem("v_pads_set"),
                                                       sem("ident_ready"))
        w_turned, w_copied = sem("w_turned"), sem("w_copied")
        stats_ready, mean_ready, stats2_ready, mean2_ready = (sem("stats_ready"), sem("mean_ready"),
                                                              sem("stats2_ready"), sem("mean2_ready"))
        var_ready, rstd_ready, xn_ready, bo_added = sem("var_ready"), sem("rstd_ready"), sem("xn_ready"), sem("bo_added")
        xn_turned, xn_copied, qk_done, v_done = sem("xn_turned"), sem("xn_copied"), sem("qk_done"), sem("v_done")
        qk_biased, v_biased = sem("qk_biased"), sem("v_biased")
        rope_mul, rope_done = sem("rope_mul"), sem("rope_done")
        p1_ready, rest_ready, p2_ready, p3_ready = (sem("p1_ready"), sem("rest_ready"),
                                                    sem("p2_ready"), sem("p3_ready"))
        p1_spread, rope_cos_done, stack_turned = sem("p1_spread"), sem("rope_cos_done"), sem("stack_turned")
        stack_dve, stack_act = sem("stack_dve"), sem("stack_act")
        exponent_ready, magic_ready, piece_cut = sem("exponent_ready"), sem("magic_ready"), sem("piece_cut")
        piece_checked, piece_rounded = sem("piece_checked"), sem("piece_rounded")
        max_scored, max_taken = sem("max_scored"), sem("max_taken")
        far_scored, far_taken = sem("far_scored"), sem("far_taken")
        neg_ready, shift_turned, shift_copied = sem("neg_ready"), sem("shift_turned"), sem("shift_copied")
        scored, exp_done, masked = sem("scored"), sem("exp_done"), sem("masked")
        pv_done, o_copied, o_turned, normed = sem("pv_done"), sem("o_copied"), sem("o_turned"), sem("normed")
        attn_turned, attn_copied = sem("attn_turned"), sem("attn_copied")
        projected, resid_done = sem("projected"), sem("resid_done")
        var2_ready, rstd2_ready, xn2_ready = sem("var2_ready"), sem("rstd2_ready"), sem("xn2_ready")
        xn2_turned, xh_ready, xl_ready = sem("xn2_turned"), sem("xh_ready"), sem("xl_ready")
        gate_done, tanh_done, gated_done = sem("gate_done"), sem("tanh_done"), sem("gated_done")
        up_done, fuse_done = sem("up_done"), sem("fuse_done")
        fh_ready, fl_ready, down_done = sem("fh_ready"), sem("fl_ready"), sem("down_done")
        scaled_done, out_ready = sem("scaled_done"), sem("out_ready")
        dve_step = sem("dve_step")

        block = ctx.enter_context(nc.Block())

        w_dst = [w_gate, w_up, w_down]
        piece_width = [min(WP, w_dst[m].shape[2] - c0) for m, _, c0 in weight_pieces]

        def heads(buf, n, side):
            return buf[:, n % 2, side * E:(side + 1) * E].rearrange("p (h d) -> p h d", d=D)

        def blocks(n, side, which):
            return parts[:, n % 2, side * H:(side + 1) * H, which[side], :]

        def spread(src, dst):
            return src if dst.shape[2] == 1 else src.to_broadcast(dst.shape)

        def one(buf, n, side):
            return heads(buf, n, side).unsqueeze(2)

        def stack_copy(n):
            t, b = divmod(n, 4)
            return ((q_stack, k_stack)[b // 2][0:STACK, 8 * (b % 2):8 * (b % 2) + 8, t * P:(t + 1) * P],
                    ps[0:STACK, banks_of["turn_stack", n][0], :].bitcast(bf16).rearrange("p (h s) -> p h s", h=8))

        def dve_stacks(tiles):
            return len([n for n in STACKS_BY_DVE if n < 4 * tiles])

        def unit_of_far(n):
            return max(u for u in range(len(units)) if first_far[u] <= n)

        @block.sync
        def _(sp):
            def load_x(n):
                t0, t1 = X_LOADS[n]
                sp.dma_start(x_sb[:, t0:t1, :], x[0, t0 * P:t1 * P, :].rearrange("(t p) e -> p t e", p=P)
                             ).then_inc(x_in[n], 16)

            def load_w(n):
                sp.dma_start(w_in[:, n, :, :], (Wq, Wk, Wv, Wo)[n].rearrange("(b p) e -> p b e", p=P)
                             ).then_inc(qkv_w_in[n] if n < 3 else wo_in, 16)

            def load_bias(n):
                sp.dma_start(bias_bc[:, n * E:(n + 1) * E],
                             (bq, bk, bv)[n].rearrange("(a n) -> a n", a=1).to_broadcast([P, E])).then_inc(bias_in, 16)

            load_x(0)
            load_w(0)
            load_x(1)
            load_bias(0)
            load_bias(1)
            load_w(2)
            load_bias(2)
            sp.dma_start(cos_sb[:, :, :], cos_t.rearrange("(t p) d -> p t d", p=P)).then_inc(rope_in, 16)
            sp.dma_start(sin_sb[:, :, :], sin_t.rearrange("(t p) d -> p t d", p=P)).then_inc(rope_in, 16)
            load_x(2)
            load_x(3)
            sp.dma_start(bo_bc[:, :], bo.rearrange("(a n) -> a n", a=1).to_broadcast([P, E])).then_inc(bo_in, 16)
            load_w(3)
            sp.dma_start(causal_sb[:, :], causal).then_inc(mask_in, 16)
            sp.dma_start(down_bc[:, :], down_scale.rearrange("(a n) -> a n", a=1).to_broadcast([P, E])).then_inc(scale_in, 16)
            sp.dma_start(gate_col[:, :], gate_scale.rearrange("(a p) -> p a", p=P),
                         allow_slow_non_contiguous=True).then_inc(scale_in, 16)
            sp.dma_start(up_col[:, :], up_scale.rearrange("(a p) -> p a", p=P),
                         allow_slow_non_contiguous=True).then_inc(scale_in, 16)
            sp.wait_ge(ones_set, 1)
            sp.dma_start(k_stack[STACK:ROWS, :, :],
                         ones_row[:, :].unsqueeze(1).to_broadcast([2, H, S])).then_inc(ones_in, 16)
            for step in order["sync"]:
                kind, n = step
                if kind == "raw":
                    m, kt, c0 = weight_pieces[n]
                    if n >= 2:
                        sp.wait_ge(piece_rounded, n - 1)
                    sp.dma_start(w_raw[:, n % 2, 0:piece_width[n]],
                                 (gate_w, up_w, down_w)[m][kt * P:(kt + 1) * P, c0:c0 + piece_width[n]]
                                 ).then_inc(raw_in[n % 2], 16)
                elif kind == "shift_in":
                    c, g = units[n]
                    sp.wait_ge(shift_copied, n + 1)
                    for p in range(2):
                        sp.dma_start(q_stack[STACK + p:STACK + p + 1, g * G:(g + 1) * G, c * C:(c + 1) * C],
                                     max_rows[p * G:(p + 1) * G, n % 2, :]).then_inc(shift_in[n], 16)
                elif kind == "store":
                    t = 2 * n
                    sp.wait_ge(out_ready, n + 1)
                    sp.dma_start(out[0, t * P:(t + 2) * P, :].rearrange("(t p) e -> p t e", p=P),
                                 out_sb[:, n % 2, :, :]).then_inc(stored[n], 16)
            for s in stored:
                sp.wait_ge(s, 16)

        @block.gpsimd
        def _(pool):
            nc.gpsimd.memset(warm[:, :], 0.0).then_inc(warm_set, 1)
            nc.gpsimd.memset(minus_half[:, :], -0.5).then_inc(half_set, 1)
            pool.wait_ge(half_set, 1)
            nc.gpsimd.memset(ones_row[:, :], 1.0).then_inc(ones_set, 1)
            pool.wait_ge(ones_set, 1)
            for step in order["gpsimd"]:
                kind, n = step[:2]
                if kind == "power":
                    pool.wait_ge(var_ready, n + 1)
                    nc.gpsimd.tensor_tensor(rstd[:, n % 2, :], var_eps[:, n % 2, :], minus_half[:, :],
                                            ALU.pow).then_inc(rstd_ready, 1)
                elif kind == "bo":
                    if n == 0:
                        pool.wait_ge(bo_in, 16)
                    pool.wait_ge(xn_ready, n + 1)
                    nc.gpsimd.tensor_tensor(x_sb[:, n, :], x_sb[:, n, :], bo_bc[:, :], ALU.add).then_inc(bo_added, 1)
                elif kind == "rope":
                    if n == 0:
                        pool.wait_ge(rope_in, 32)
                    pool.wait_ge(qk_biased, n + 1)
                    if n >= 2:
                        pool.wait_ge(rope_done, n - 1)
                    v = qk[:, n % 2, :].rearrange("p (h i two) -> p h i two", two=2, i=D // 2)
                    o = qk_sin[:, n % 2, :].rearrange("p (h i two) -> p h i two", two=2, i=D // 2)
                    s = sin_sb[:, n, :].rearrange("p (i two) -> p i two", two=2)
                    if n not in COS_BY_DVE:
                        nc.gpsimd.tensor_tensor(qk_cos[:, n % 2, :].rearrange("p (h d) -> p h d", d=D),
                                                qk[:, n % 2, :].rearrange("p (h d) -> p h d", d=D),
                                                cos_sb[:, n, :].unsqueeze(1).to_broadcast([P, 2 * H, D]), ALU.mult)
                    for a in range(2):
                        last = nc.gpsimd.tensor_tensor(o[:, :, :, a], v[:, :, :, 1 - a],
                                                       s[:, :, a].unsqueeze(1).to_broadcast([P, 2 * H, D // 2]), ALU.mult)
                    last.then_inc(rope_mul, 1)
                elif kind == "p3":
                    pool.wait_ge(p2_ready, n + 1)
                    for side in range(2):
                        last = nc.gpsimd.tensor_tensor(blocks(n, side, P3_BLOCKS), one(rest, n, side),
                                                       blocks(n, side, P2_FIRST), ALU.subtract)
                    last.then_inc(p3_ready, 1)
                elif kind == "round":
                    raw, e = w_raw[:, n % 2, 0:piece_width[n]], w_exp[:, n % 2, 0:piece_width[n]]
                    pool.wait_ge(magic_ready, n + 1)
                    nc.gpsimd.tensor_tensor(raw, raw, e, ALU.add).then_inc(piece_cut, 1)
                    pool.wait_ge(piece_cut, 2 * n + 1)
                    nc.gpsimd.tensor_tensor(raw, raw, e, ALU.subtract).then_inc(piece_cut, 1)
                elif kind == "rounded":
                    m, kt, c0 = weight_pieces[n]
                    w = piece_width[n]
                    pool.wait_ge(piece_checked, n + 1)
                    nc.gpsimd.tensor_tensor(w_dst[m][:, kt, c0:c0 + w], w_raw[:, n % 2, 0:w], w_chk[:, 0:w],
                                            ALU.add).then_inc(piece_rounded, 1)
                elif kind == "mask":
                    v, j = step[1:]
                    c, g = second[v]
                    i = j - TC * c
                    k = first_pv[v] + j
                    pool.wait_ge(exp_done, 2 * (k + 1))
                    block_ = probs[:, k % 2, :, i * P:(i + 1) * P]
                    nc.gpsimd.affine_select(out=block_, in_=block_, compare_op=ALU.is_ge, fill=0.0, base=0,
                                            pattern=[[0, G], [1, P]], channel_multiplier=-1).then_inc(masked, 1)
                elif kind == "power2":
                    pool.wait_ge(var2_ready, n + 1)
                    nc.gpsimd.tensor_tensor(rstd2[:, n % 2, :], var_eps2[:, n % 2, :], minus_half[:, :],
                                            ALU.pow).then_inc(rstd2_ready, 1)
                elif kind == "fl":
                    pool.wait_ge(fh_ready, n + 1)
                    nc.gpsimd.tensor_tensor(fl[:, n % 2, :], fuse[:, n % 2, :], fh[:, n % 2, :].bitcast(fp32),
                                            ALU.subtract).then_inc(fl_ready, 1)
                elif kind == "out":
                    pool.wait_ge(scaled_done, n + 1)
                    if n >= 2:
                        pool.wait_ge(stored[n - 2], 16)
                    nc.gpsimd.tensor_tensor(out_sb[:, n % 2, :, :], scaled[:, n % 2, :, :],
                                            x_sb[:, 2 * n:2 * n + 2, :], ALU.add).then_inc(out_ready, 1)

        @block.scalar
        def _(act):
            act.dma_start(ident_sb[:, :], ident).then_inc(ident_in, 16)
            act.dma_start(w_in[:, 1, :, :], Wk.rearrange("(b p) e -> p b e", p=P)).then_inc(qkv_w_in[1], 16)
            act.wait_ge(warm_set, 1)
            nc.scalar.activation(exp_of_zero[:, :], warm[0:1, 0:1], ACT.Exp)
            act.wait_ge(ident_in, 16)
            nc.scalar.copy(ident_bf[:, :], ident_sb[:, :]).then_inc(ident_ready, 1)
            for step in order["scalar"]:
                kind, n = step[:2]
                if kind == "w_copy":
                    act.wait_ge(w_turned, n + 1)
                    dst = w_t[:, :, n * E:(n + 1) * E] if n < 3 else wo_t[:, :, :]
                    nc.scalar.copy(dst, ps[:, banks_of["turn_w", n][0], :].rearrange("p (k f) -> p k f", k=EK)
                                   ).then_inc(w_copied, 1)
                elif kind == "xn_copy":
                    act.wait_ge(xn_turned, n + 1)
                    if n >= 4:
                        act.wait_ge(v_done, n - 3)
                    nc.scalar.copy(xn_t[:, n % 4, :, :],
                                   ps[:, banks_of["turn_xn", n][0], 0:EK * P].rearrange("p (k s) -> p k s", k=EK)
                                   ).then_inc(xn_copied, 1)
                elif kind == "p1":
                    act.wait_ge(rope_done, n + 1)
                    if n >= 2:
                        act.wait_ge(stack_turned, 4 * (n - 1))
                    for side in range(2):
                        dst = blocks(n, side, P1_FIRST if n in SPREAD_BY_DVE else P1_BLOCKS)
                        last = nc.scalar.copy(dst, spread(one(qk_rot, n, side), dst))
                    last.then_inc(p1_ready, 1)
                elif kind == "p2":
                    act.wait_ge(rest_ready, n + 1)
                    for side in range(2):
                        dst = blocks(n, side, P2_BLOCKS)
                        last = nc.scalar.copy(dst, spread(one(rest, n, side), dst))
                    last.then_inc(p2_ready, 1)
                elif kind == "stack_act":
                    act.wait_ge(stack_turned, n + 1)
                    nc.scalar.copy(*stack_copy(n)).then_inc(stack_act, 1)
                elif kind == "exp":
                    v, m = step[1:]
                    j, pair, q0 = exps[v][m]
                    k = first_pv[v] + j
                    b0, b1 = banks_of["score", v, m]
                    act.wait_ge(scored, first_exp[v] + m + 1)
                    if k >= 2:
                        act.wait_ge(pv_done, k - 1)
                    nc.scalar.activation(probs[:, k % 2, 2 * pair:2 * pair + 2, q0:C],
                                         ps[:, b0:b1 + 1:b1 - b0, q0:C], ACT.Exp, scale=SCALE).then_inc(exp_done, 1)
                elif kind == "shift_copy":
                    act.wait_ge(shift_turned, n + 1)
                    if n >= 2:
                        act.wait_ge(shift_in[n - 2], 32)
                    nc.scalar.copy(max_rows[:, n % 2, :],
                                   ps[0:2 * G, banks_of["shift", n][0], 0:C // 2].bitcast(bf16)).then_inc(shift_copied, 1)
                elif kind == "o_copy":
                    act.wait_ge(pv_done, first_pv[n + 1])
                    if n >= 2:
                        act.wait_ge(o_turned, n - 1)
                    nc.scalar.copy(o_sb[:, n % 2, :], ps[:, banks_of["pv", n, 0][0], :]).then_inc(o_copied, 1)
                elif kind == "attn_copy":
                    act.wait_ge(attn_turned, n + 1)
                    if n >= 2:
                        act.wait_ge(projected, n - 1)
                    nc.scalar.copy(attn_t[:, n % 2, :, :],
                                   ps[:, banks_of["turn_attn", n][0], 0:EK * P].rearrange("p (k s) -> p k s", k=EK)
                                   ).then_inc(attn_copied, 1)
                elif kind == "xh":
                    c, i = divmod(n, TC)
                    act.wait_ge(xn2_turned, n + 1)
                    if c >= 1 and i == 0:
                        act.wait_ge(up_done, FK * c)
                    nc.scalar.copy(xh[:, :, i * P:(i + 1) * P],
                                   ps[:, banks_of["turn_xn2", n][0], 0:EK * P].rearrange("p (k s) -> p k s", k=EK)
                                   ).then_inc(xh_ready, 1)
                elif kind == "tanh":
                    it = n % FK
                    act.wait_ge(gate_done, n + 1)
                    if n >= 2:
                        act.wait_ge(gated_done, n - 1)
                    nc.scalar.activation(tanh_sb[:, n % 2, :], ps[:, banks_of["gate", n][0], :], ACT.Tanh,
                                         scale=half_gate[:, it:it + 1]).then_inc(tanh_done, 1)
                elif kind == "fh":
                    act.wait_ge(fuse_done, n + 1)
                    if n >= 2:
                        act.wait_ge(down_done, n - 1)
                    nc.scalar.copy(fh[:, n % 2, :], fuse[:, n % 2, :]).then_inc(fh_ready, 1)

        @block.vector
        def _(dve):
            n_steps = [0]

            def then_wait(ins):
                n_steps[0] += 1
                ins.then_inc(dve_step, 1)
                dve.wait_ge(dve_step, n_steps[0])

            nc.vector.memset(v_ones[:, :, :, D + 1:32], 0.0)
            nc.vector.memset(v_ones[:, :, :, D:D + 1], 1.0).then_inc(v_pads_set, 1)
            for step in order["vector"]:
                kind, n = step[:2]
                if kind == "stats":
                    dve.wait_ge(x_in[[t1 > n for _, t1 in X_LOADS].index(True)], 16)
                    if n >= 2:
                        dve.wait_ge(mean_ready, n - 1)
                    nc.vector.bn_stats(stats[:, n % 2, :], x_sb[:, n, :]).then_inc(stats_ready, 1)
                elif kind == "mean":
                    dve.wait_ge(stats_ready, n + 1)
                    if n >= 2:
                        dve.wait_ge(xn_ready, n - 1)
                    nc.vector.bn_aggr(mean_var[:, n % 2, :], stats[:, n % 2, :]).then_inc(mean_ready, 1)
                elif kind == "eps":
                    dve.wait_ge(mean_ready, n + 1)
                    nc.vector.tensor_scalar(var_eps[:, n % 2, :], mean_var[:, n % 2, 1:2], 1e-5, None, ALU.add).then_inc(var_ready, 1)
                elif kind == "xn":
                    dve.wait_ge(rstd_ready, n + 1)
                    if n >= 2:
                        dve.wait_ge(xn_turned, n - 1)
                    nc.vector.tensor_scalar(xn[:, n % 2, :], x_sb[:, n, :], mean_var[:, n % 2, 0:1], rstd[:, n % 2, :],
                                            ALU.subtract, ALU.mult).then_inc(xn_ready, 1)
                elif kind == "bias":
                    if n == 0:
                        dve.wait_ge(bias_in, 48)
                    dve.wait_ge(qk_done, n + 1)
                    if n >= 2:
                        dve.wait_ge(rope_mul, n - 1)
                    nc.vector.tensor_tensor(qk[:, n % 2, :], ps[:, banks_of["qk", n][0], :], bias_bc[:, 0:2 * E],
                                            ALU.add).then_inc(qk_biased, 1)
                elif kind == "bias_v":
                    dve.wait_ge(v_done, n + 1)
                    nc.vector.tensor_tensor(v_ones[:, n, :, 0:D],
                                            ps[:, banks_of["v", n][0], 0:E].rearrange("p (h d) -> p h d", d=D),
                                            bias_bc[:, 2 * E:3 * E].rearrange("p (h d) -> p h d", d=D), ALU.add).then_inc(v_biased, 1)
                elif kind == "rope_cos":
                    dve.wait_ge(qk_biased, n + 1)
                    if n == COS_BY_DVE[0]:
                        dve.wait_ge(rope_in, 32)
                    if n >= 2:
                        dve.wait_ge(rope_done, n - 1)
                    nc.vector.tensor_tensor(qk_cos[:, n % 2, :].rearrange("p (h d) -> p h d", d=D),
                                            qk[:, n % 2, :].rearrange("p (h d) -> p h d", d=D),
                                            cos_sb[:, n, :].unsqueeze(1).to_broadcast([P, 2 * H, D]),
                                            ALU.mult).then_inc(rope_cos_done, 1)
                elif kind == "rope_sum":
                    dve.wait_ge(rope_mul, n + 1)
                    if n in COS_BY_DVE:
                        dve.wait_ge(rope_cos_done, COS_BY_DVE.index(n) + 1)
                    if n >= 2:
                        dve.wait_ge(rest_ready, n - 1)
                    nc.vector.tensor_tensor(qk_rot[:, n % 2, :], qk_cos[:, n % 2, :], qk_sin[:, n % 2, :],
                                            ALU.add).then_inc(rope_done, 1)
                elif kind == "rest":
                    dve.wait_ge(p1_ready, n + 1)
                    if n >= 2:
                        dve.wait_ge(p3_ready, n - 1)
                    for side in range(2):
                        last = nc.vector.tensor_tensor(one(rest, n, side), one(qk_rot, n, side),
                                                       blocks(n, side, P1_FIRST), ALU.subtract)
                    last.then_inc(rest_ready, 1)
                elif kind == "spread":
                    dve.wait_ge(p1_ready, n + 1)
                    for side in range(2):
                        dst = blocks(n, side, P1_OTHERS)
                        last = nc.vector.tensor_copy(dst, spread(blocks(n, side, P1_FIRST), dst))
                    last.then_inc(p1_spread, 1)
                elif kind == "stack_dve":
                    dve.wait_ge(stack_turned, n + 1)
                    nc.vector.tensor_copy(*stack_copy(n)).then_inc(stack_dve, 1)
                elif kind == "exponent":
                    w = piece_width[n]
                    dve.wait_ge(raw_in[n % 2], 16 * (n // 2 + 1))
                    if n >= 2:
                        dve.wait_ge(piece_cut, 2 * (n - 1))
                    nc.vector.tensor_scalar(w_exp[:, n % 2, 0:w].bitcast(i32), w_raw[:, n % 2, 0:w].bitcast(i32),
                                            0x7F800000, None, ALU.bitwise_and).then_inc(exponent_ready, 1)
                elif kind == "magic":
                    w = piece_width[n]
                    dve.wait_ge(exponent_ready, n + 1)
                    nc.vector.tensor_scalar(w_exp[:, n % 2, 0:w], w_exp[:, n % 2, 0:w], 2.0 ** -6, 1.5 * 2.0 ** 20,
                                            ALU.max, ALU.mult).then_inc(magic_ready, 1)
                elif kind == "check":
                    w = piece_width[n]
                    dve.wait_ge(piece_cut, 2 * (n + 1))
                    if n >= 1:
                        dve.wait_ge(piece_rounded, n)
                    nc.vector.tensor_scalar(w_chk[:, 0:w], w_raw[:, n % 2, 0:w], float(np.finfo(np.float32).max) / 464.0,
                                            0.0, ALU.mult, ALU.mult).then_inc(piece_checked, 1)
                elif kind == "taken":
                    u, m = step[1:]
                    h, t, k0, w, diagonal = pieces[u][m]
                    k = first_piece[u] + m
                    col = (t % TC) * G + h
                    bank = banks_of["max", u, m][0]
                    if k == 0:
                        dve.wait_ge(mask_in, 16)
                    if m == 0 and u >= 2:
                        dve.wait_ge(neg_ready, u - 1)
                    if k >= 4 and k % 2 == 0:
                        dve.wait_ge(max_taken, k - 2)
                    dve.wait_ge(max_scored, k + 1)
                    if diagonal:
                        nc.vector.tensor_tensor_reduce(
                            out=max_junk[:, k % 4, 0:w], in0=ps[:, bank, 0:w], in1=causal_sb[:, C - w:C],
                            scale=1.0, scalar=-3.0e38, op0=ALU.add, op1=ALU.max,
                            accum_out=maxes[:, u % 2, k0 // C, col:col + 1]).then_inc(max_taken, 1)
                    else:
                        nc.vector.reduce_max(maxes[:, u % 2, k0 // C, col:col + 1], ps[:, bank, 0:w],
                                             AX.X).then_inc(max_taken, 1)
                elif kind == "far_taken":
                    u = unit_of_far(n)
                    t, pair = far[u][n - first_far[u]]
                    col = (t % TC) * G + 2 * pair
                    b = banks_of["far", n][0]
                    dve.wait_ge(far_scored, n + 1)
                    if n == first_far[u]:
                        dve.wait_ge(neg_ready, u - 1)
                    nc.vector.reduce_max(maxes[:, u % 2, 0, col:col + 2], ps[:, b:b + 2, :], AX.X).then_inc(far_taken, 1)
                elif kind == "neg":
                    c, i = units[n][0], n % 2
                    if first_far[n + 1]:
                        dve.wait_ge(far_taken, first_far[n + 1])
                    dve.wait_ge(max_taken, first_piece[n + 1])
                    top = maxes[:, i, 0, :]
                    if c >= 1:
                        then_wait(nc.vector.tensor_tensor(max_all[:, i, :], maxes[:, i, 0, :], maxes[:, i, 1, :], ALU.max))
                        top = max_all[:, i, :]
                    if n >= 2:
                        dve.wait_ge(shift_turned, n - 1)
                    top = top.rearrange("p (t h) -> p t h", h=G)
                    then_wait(nc.vector.tensor_scalar(neg_max[:, i, :, 0, :], top, -1.0, None, ALU.mult))
                    nc.vector.scalar_tensor_tensor(neg_max[:, i, :, 1, :], top, -1.0, neg_max[:, i, :, 0, :],
                                                   ALU.mult, ALU.subtract).then_inc(neg_ready, 1)
                elif kind == "norm":
                    c, g = second[n]
                    o = ps[:, banks_of["turn_o", n][0], :].rearrange("p (t h d) -> p t h d", h=G, d=32)
                    dve.wait_ge(o_turned, n + 1)
                    then_wait(nc.vector.reciprocal(inv_sum[:, n % 2, :, :], o[:, :, :, D]))
                    nc.vector.tensor_tensor(attn_s[:, TC * c:TC * (c + 1), g * G * D:(g + 1) * G * D]
                                            .rearrange("p t (h d) -> p t h d", d=D), o[:, :, :, 0:D],
                                            inv_sum[:, n % 2, :, :].unsqueeze(3).to_broadcast([P, TC, G, D]),
                                            ALU.mult).then_inc(normed, 1)
                elif kind == "resid":
                    dve.wait_ge(projected, n + 1)
                    dve.wait_ge(bo_added, n + 1)
                    nc.vector.tensor_tensor(x_sb[:, n, :], x_sb[:, n, :], ps[:, banks_of["project", n][0], 0:E],
                                            ALU.add).then_inc(resid_done, 1)
                elif kind == "stats2":
                    dve.wait_ge(resid_done, n + 1)
                    if n >= 2:
                        dve.wait_ge(mean2_ready, n - 1)
                    nc.vector.bn_stats(stats2[:, n % 2, :], x_sb[:, n, :]).then_inc(stats2_ready, 1)
                elif kind == "mean2":
                    dve.wait_ge(stats2_ready, n + 1)
                    if n >= 2:
                        dve.wait_ge(xn2_ready, n - 1)
                    nc.vector.bn_aggr(mean_var2[:, n % 2, :], stats2[:, n % 2, :]).then_inc(mean2_ready, 1)
                elif kind == "eps2":
                    dve.wait_ge(mean2_ready, n + 1)
                    nc.vector.tensor_scalar(var_eps2[:, n % 2, :], mean_var2[:, n % 2, 1:2], 1e-5, None, ALU.add).then_inc(var2_ready, 1)
                elif kind == "xn2":
                    dve.wait_ge(rstd2_ready, n + 1)
                    if n >= 2:
                        dve.wait_ge(xn2_turned, n - 1)
                    nc.vector.tensor_scalar(xn2[:, n % 2, :], x_sb[:, n, :], mean_var2[:, n % 2, 0:1], rstd2[:, n % 2, :],
                                            ALU.subtract, ALU.mult).then_inc(xn2_ready, 1)
                elif kind == "xl":
                    c, i = divmod(n, TC)
                    dve.wait_ge(xh_ready, n + 1)
                    nc.vector.tensor_tensor(xl[:, :, i * P:(i + 1) * P],
                                            ps[:, banks_of["turn_xn2", n][0], 0:EK * P].rearrange("p (k s) -> p k s", k=EK),
                                            xh[:, :, i * P:(i + 1) * P].bitcast(fp32), ALU.subtract).then_inc(xl_ready, 1)
                elif kind == "gated":
                    dve.wait_ge(tanh_done, n + 1)
                    if n >= 2:
                        dve.wait_ge(fuse_done, n - 1)
                    nc.vector.scalar_tensor_tensor(gated[:, n % 2, :], tanh_sb[:, n % 2, :], 1.0,
                                                   ps[:, banks_of["gate", n][0], :], ALU.add, ALU.mult).then_inc(gated_done, 1)
                elif kind == "fuse":
                    it = n % FK
                    if n == 0:
                        then_wait(nc.vector.tensor_tensor(half_gu[:, :], half_gate[:, :], up_col[:, :], ALU.mult))
                    dve.wait_ge(up_done, n + 1)
                    dve.wait_ge(gated_done, n + 1)
                    if n >= 2:
                        dve.wait_ge(fl_ready, n - 1)
                    nc.vector.scalar_tensor_tensor(fuse[:, n % 2, :], gated[:, n % 2, :], half_gu[:, it:it + 1],
                                                   ps[:, banks_of["up", n][0], :], ALU.mult, ALU.mult).then_inc(fuse_done, 1)
                elif kind == "scaled":
                    c, b = divmod(n, 2)
                    dve.wait_ge(down_done, FK * (c + 1))
                    if n >= 2:
                        dve.wait_ge(out_ready, n - 1)
                    nc.vector.tensor_tensor(scaled[:, b, :, :],
                                            ps[:, banks_of["down", FK * c][b], :].rearrange("p (t e) -> p t e", t=2),
                                            down_bc[:, :].unsqueeze(1).to_broadcast([P, 2, E]), ALU.mult).then_inc(scaled_done, 1)
                if step == ("bias", T - 1):
                    dve.wait_ge(scale_in, 48)
                    then_wait(nc.vector.tensor_scalar(half_gate[:, :], gate_col[:, :], 0.5, None, ALU.mult))

        @block.tensor
        def _(pe):
            empties = {"w_copy": w_copied, "xn_copy": xn_copied, "bias": qk_biased,
                       "bias_v": v_biased, "shift_copy": shift_copied, "far_taken": far_taken, "o_copy": o_copied, "norm": normed,
                       "attn_copy": attn_copied, "resid": resid_done, "xl": xl_ready, "gated": gated_done,
                       "fuse": fuse_done,
                       "scaled": scaled_done}

            def emptied(step):
                if step[0] == "taken":
                    return max_taken, first_piece[step[1]] + step[2] + 1
                if step[0] == "exp":
                    return exp_done, first_exp[step[1]] + step[2] + 1
                if step[0] == "stack_dve":
                    return stack_dve, len([n for n in STACKS_BY_DVE if n <= step[1]])
                if step[0] == "stack_act":
                    return stack_act, step[1] + 1 - len([n for n in STACKS_BY_DVE if n <= step[1]])
                return empties[step[0]], step[1] + 1

            pe.wait_ge(warm_set, 1)
            for step in order["tensor"]:
                kind, n = step[:2]
                for _ in range(WARM_UP.get(step, 0)):
                    nc.tensor.matmul(ps[:, 7, :], warm[:, 0:P], warm[:, :], start=True, stop=True)
                bank = banks_of.get(step, [None])
                for last_user in former.get(step, []):
                    if last_user:
                        pe.wait_ge(*emptied(last_user))
                if kind == "turn_w":
                    if n == 0:
                        pe.wait_ge(ident_in, 16)
                    pe.wait_ge(qkv_w_in[n] if n < 3 else wo_in, 16)
                    for k in range(EK):
                        for b in range(EK):
                            o = (k * EK + b) * P
                            last = nc.tensor.transpose(ps[:, bank[0], o:o + P], w_in[:, n, b, k * P:(k + 1) * P], ident_sb[:, :])
                    last.then_inc(w_turned, 1)
                elif kind == "turn_xn":
                    if n == 0:
                        pe.wait_ge(ident_in, 16)
                    pe.wait_ge(xn_ready, n + 1)
                    for k in range(EK):
                        last = nc.tensor.transpose(ps[:, bank[0], k * P:(k + 1) * P], xn[:, n % 2, k * P:(k + 1) * P], ident_sb[:, :])
                    last.then_inc(xn_turned, 1)
                elif kind == "qk":
                    pe.wait_ge(xn_copied, n + 1)
                    if n == 0:
                        pe.wait_ge(w_copied, 2)
                    for k in range(EK):
                        last = nc.tensor.matmul(ps[:, bank[0], :], xn_t[:, n % 4, k, :], w_t[:, k, 0:2 * E],
                                                start=(k == 0), stop=(k == EK - 1))
                    last.then_inc(qk_done, 1)
                elif kind == "v":
                    if n == 0:
                        pe.wait_ge(w_copied, 3)
                    for k in range(EK):
                        last = nc.tensor.matmul(ps[:, bank[0], 0:E], xn_t[:, n % 4, k, :], w_t[:, k, 2 * E:3 * E],
                                                start=(k == 0), stop=(k == EK - 1))
                    last.then_inc(v_done, 1)
                elif kind == "turn_stack":
                    t, b = divmod(n, 4)
                    if n == 0:
                        pe.wait_ge(ident_ready, 1)
                    pe.wait_ge(p3_ready, t + 1)
                    if t in SPREAD_BY_DVE:
                        pe.wait_ge(p1_spread, SPREAD_BY_DVE.index(t) + 1)
                    o = ps[0:STACK, bank[0], :].bitcast(bf16)
                    for h in range(8):
                        last = nc.tensor.transpose(o[:, h * P:(h + 1) * P],
                                                   parts[:, t % 2, 8 * b + h, :, :].rearrange("p b d -> p (b d)"),
                                                   ident_bf[:, :])
                    last.then_inc(stack_turned, 1)
                elif kind == "max":
                    u, m = step[1:]
                    c, g = units[u]
                    h, t, k0, w, _ = pieces[u][m]
                    if g == 0 and (m == 0 or pieces[u][m - 1][1] != t):
                        if dve_stacks(t + 1):
                            pe.wait_ge(stack_dve, dve_stacks(t + 1))
                        if 4 * (t + 1) > dve_stacks(t + 1):
                            pe.wait_ge(stack_act, 4 * (t + 1) - dve_stacks(t + 1))
                    nc.tensor.matmul(ps[:, bank[0], 0:w], q_stack[0:STACK, g * G + h, t * P:(t + 1) * P],
                                     k_stack[0:STACK, g * G + h, k0:k0 + w], start=True, stop=True).then_inc(max_scored, 1)
                elif kind == "far":
                    u = unit_of_far(n)
                    g = units[u][1]
                    t, pair = far[u][n - first_far[u]]
                    if n == 0:
                        if dve_stacks(T):
                            pe.wait_ge(stack_dve, dve_stacks(T))
                        pe.wait_ge(stack_act, 4 * T - dve_stacks(T))
                    for i in range(2):
                        h = g * G + 2 * pair + i
                        last = nc.tensor.matmul(ps[:, bank[i], :], q_stack[0:STACK, h, t * P:(t + 1) * P],
                                                k_stack[0:STACK, h, 0:C], start=True, stop=True)
                    last.then_inc(far_scored, 1)
                elif kind == "shift":
                    pe.wait_ge(neg_ready, n + 1)
                    for i in range(TC):
                        last = nc.tensor.transpose(ps[0:2 * G, bank[0], i * P // 2:(i + 1) * P // 2].bitcast(bf16),
                                                   neg_max[:, n % 2, i, :, :].rearrange("p a h -> p (a h)"), ident_bf[:, :])
                    last.then_inc(shift_turned, 1)
                elif kind == "score":
                    v, m = step[1:]
                    c, g = second[v]
                    j, pair, q0 = exps[v][m]
                    if m == 0:
                        if v == 0:
                            pe.wait_ge(ones_in, 16)
                        pe.wait_ge(shift_in[SECOND_PASS[v]], 32)
                    for i in range(2):
                        h = g * G + 2 * pair + i
                        last = nc.tensor.matmul(ps[:, bank[i], q0:C], k_stack[0:ROWS, h, j * P:(j + 1) * P],
                                                q_stack[0:ROWS, h, c * C + q0:(c + 1) * C], start=True, stop=True)
                    last.then_inc(scored, 1)
                elif kind == "pv":
                    v, j = step[1:]
                    c, g = second[v]
                    k = first_pv[v] + j
                    q0 = max(0, (j - TC * c) * P)
                    o = banks_of["pv", v, 0][0]
                    if k == 0:
                        pe.wait_ge(v_pads_set, 1)
                    if j == 0:
                        pe.wait_ge(v_biased, TC * (c + 1))
                    pe.wait_ge(exp_done, 2 * (k + 1))
                    if j >= TC * c:
                        pe.wait_ge(masked, TC * v + j - TC * c + 1)
                    for h in range(G):
                        last = nc.tensor.matmul(ps[32 * h:32 * h + 32, o, q0:C], v_ones[:, j, g * G + h, :],
                                                probs[:, k % 2, h, q0:C], start=(j == 0), stop=(j == TC * (c + 1) - 1))
                    last.then_inc(pv_done, 1)
                elif kind == "turn_o":
                    pe.wait_ge(o_copied, n + 1)
                    for i in range(TC):
                        last = nc.tensor.transpose(ps[:, bank[0], i * P:(i + 1) * P], o_sb[:, n % 2, i * P:(i + 1) * P], ident_sb[:, :])
                    last.then_inc(o_turned, 1)
                elif kind == "turn_attn":
                    if n == 0:
                        if dve_stacks(T):
                            pe.wait_ge(stack_dve, dve_stacks(T))
                        pe.wait_ge(stack_act, 4 * T - dve_stacks(T))
                    pe.wait_ge(normed, chunk_done(units, n // TC))
                    for k in range(EK):
                        last = nc.tensor.transpose(ps[:, bank[0], k * P:(k + 1) * P], attn_s[:, n, k * P:(k + 1) * P], ident_sb[:, :])
                    last.then_inc(attn_turned, 1)
                elif kind == "project":
                    pe.wait_ge(attn_copied, n + 1)
                    if n == 0:
                        pe.wait_ge(w_copied, 4)
                    for k in range(EK):
                        last = nc.tensor.matmul(ps[:, bank[0], 0:E], attn_t[:, n % 2, k, :], wo_t[:, k, :],
                                                start=(k == 0), stop=(k == EK - 1))
                    last.then_inc(projected, 1)
                elif kind == "turn_xn2":
                    pe.wait_ge(xn2_ready, n + 1)
                    for k in range(EK):
                        last = nc.tensor.transpose(ps[:, bank[0], k * P:(k + 1) * P], xn2[:, n % 2, k * P:(k + 1) * P], ident_sb[:, :])
                    last.then_inc(xn2_turned, 1)
                elif kind in ("gate", "up"):
                    c, it = divmod(n, FK)
                    if kind == "gate" and it == 0:
                        pe.wait_ge(xh_ready, TC * (c + 1))
                        pe.wait_ge(xl_ready, TC * (c + 1))
                    if kind == "gate" and n == 0:
                        pe.wait_ge(piece_rounded, len(weight_pieces))
                    w, done = (w_gate, gate_done) if kind == "gate" else (w_up, up_done)
                    for k in range(EK):
                        for a, xs in enumerate((xh, xl)):
                            last = nc.tensor.matmul(ps[:, bank[0], :], w[:, k, it * P:(it + 1) * P], xs[:, k, :],
                                                    start=(k == 0 and a == 0), stop=(k == EK - 1 and a == 1))
                    last.then_inc(done, 1)
                elif kind == "down":
                    c, it = divmod(n, FK)
                    o = banks_of["down", FK * c]
                    pe.wait_ge(fh_ready, n + 1)
                    pe.wait_ge(fl_ready, n + 1)
                    for i in range(TC):
                        for a, fs in enumerate((fh, fl)):
                            last = nc.tensor.matmul(ps[:, o[i // 2], (i % 2) * E:(i % 2 + 1) * E],
                                                    fs[:, n % 2, i * P:(i + 1) * P], w_down[:, it, :],
                                                    start=(it == 0 and a == 0 and i % 2 == 0),
                                                    stop=(it == FK - 1 and a == 1), skip_group_check=True)
                    last.then_inc(down_done, 1)


_INS = ['L0_attn_x', 'L0_attn_Wq', 'L0_attn_bq', 'L0_attn_Wk', 'L0_attn_bk', 'L0_attn_Wv', 'L0_attn_bv',
        'L0_attn_Wo', 'L0_attn_bo', 'L0_ffn_gate_w', 'L0_ffn_up_w', 'L0_ffn_down_w', 'L0_ffn_gate_scale',
        'L0_ffn_up_scale', 'L0_ffn_down_scale']


def _constants():
    S, D, C = 1024, 16, 512
    pos = np.arange(S, dtype=np.float32)[:, None]
    theta = np.repeat(-np.arange(0, D, 2, dtype=np.float32) / np.float32(D), 2)
    angles = pos * np.power(np.float32(10000.0), theta)[None, :]
    sign = np.where(np.arange(D) % 2 == 0, -1.0, 1.0).astype(np.float32)
    causal = np.zeros((P, C), np.float32)
    causal[:, C - P:] = np.where(np.arange(P)[None, :] > np.arange(P)[:, None], -3.0e38, 0.0)
    return {"cos": np.cos(angles), "sin": np.sin(angles) * sign, "causal": causal,
            "ident": np.eye(P, dtype=np.float32)}


def kernel(**inputs):
    import concourse.bacc as _bacc
    from concourse.bass_utils import run_bass_kernel_spmd as _run

    nc = _bacc.Bacc("TRN2", target_bir_lowering=False, num_devices=1)
    arrays, args = {}, []
    for name, a in [(n, inputs[n]) for n in _INS] + list(_constants().items()):
        a = np.ascontiguousarray(a)
        arrays[f"in_{name}_dram"] = a
        args.append(nc.dram_tensor(f"in_{name}_dram", a.shape, mybir.dt.from_np(a.dtype), kind="ExternalInput").ap())
    out = nc.dram_tensor("out_0_dram", (1, 1024, 256), mybir.dt.float32, kind="ExternalOutput").ap()
    build(nc, *args, out)
    r = _run(nc, [arrays], core_ids=[0])
    return r.results[0]["out_0_dram"]
```
